# Optimizing a Trainium2 kernel written in Bass

```python
import numpy as np
import jax
import jax.numpy as jnp

def _softmax(x, axis=-1):
    return jax.nn.softmax(x, axis=axis)

def _gelu(x):
    return jax.nn.gelu(x, approximate=True)

def _silu(x):
    return jax.nn.silu(x)

def _sigmoid(x):
    return jax.nn.sigmoid(x)

def _layernorm(x, axis=-1, eps=1e-05):
    m = jnp.mean(x, axis=axis, keepdims=True)
    v = jnp.var(x, axis=axis, keepdims=True)
    return (x - m) / jnp.sqrt(v + eps)

def _scatter_add(tgt, idx, src, axis=0):
    return tgt.at[idx].add(src)

def _segment_sum(src, seg, n):
    return jax.ops.segment_sum(src, seg, n)
kernel_name = 'mk_dlrm_tower_d1_rec_r8_e8f7d6'

def setup_inputs(seed: int=0):
    np.random.seed(seed)
    _w = jnp.asarray

    def _rec_inputs():
        import jax
        import jax.numpy as jnp
        _tk = jax.random.key(seed)
        dense_ctx = jax.random.normal(jax.random.fold_in(_tk, 190), (2048, 16), jnp.float32)
        ids = jnp.stack([jax.random.randint(jax.random.fold_in(_tk, 200 + f), (2048,), 0, v, jnp.int32) for f, v in enumerate([1250, 125000, 1000, 1250, 1250, 12500, 12500, 1250, 125000, 1250, 1000, 1250, 12500, 125000, 1250, 12500, 1250, 1250, 125000, 125000, 1250, 12500, 12500, 1250, 1250, 1250])], axis=1)
        tbl_0 = 0.05 * jax.random.normal(jax.random.fold_in(_tk, 500 + 0), (1250, 32), jnp.float32)
        tbl_1 = 0.05 * jax.random.normal(jax.random.fold_in(_tk, 500 + 1), (125000, 32), jnp.float32)
        tbl_2 = 0.05 * jax.random.normal(jax.random.fold_in(_tk, 500 + 2), (1000, 32), jnp.float32)
        tbl_3 = 0.05 * jax.random.normal(jax.random.fold_in(_tk, 500 + 3), (1250, 32), jnp.float32)
        tbl_4 = 0.05 * jax.random.normal(jax.random.fold_in(_tk, 500 + 4), (1250, 32), jnp.float32)
        tbl_5 = 0.05 * jax.random.normal(jax.random.fold_in(_tk, 500 + 5), (12500, 32), jnp.float32)
        tbl_6 = 0.05 * jax.random.normal(jax.random.fold_in(_tk, 500 + 6), (12500, 32), jnp.float32)
        tbl_7 = 0.05 * jax.random.normal(jax.random.fold_in(_tk, 500 + 7), (1250, 32), jnp.float32)
        tbl_8 = 0.05 * jax.random.normal(jax.random.fold_in(_tk, 500 + 8), (125000, 32), jnp.float32)
        tbl_9 = 0.05 * jax.random.normal(jax.random.fold_in(_tk, 500 + 9), (1250, 32), jnp.float32)
        tbl_10 = 0.05 * jax.random.normal(jax.random.fold_in(_tk, 500 + 10), (1000, 32), jnp.float32)
        tbl_11 = 0.05 * jax.random.normal(jax.random.fold_in(_tk, 500 + 11), (1250, 32), jnp.float32)
        tbl_12 = 0.05 * jax.random.normal(jax.random.fold_in(_tk, 500 + 12), (12500, 32), jnp.float32)
        tbl_13 = 0.05 * jax.random.normal(jax.random.fold_in(_tk, 500 + 13), (125000, 32), jnp.float32)
        tbl_14 = 0.05 * jax.random.normal(jax.random.fold_in(_tk, 500 + 14), (1250, 32), jnp.float32)
        tbl_15 = 0.05 * jax.random.normal(jax.random.fold_in(_tk, 500 + 15), (12500, 32), jnp.float32)
        tbl_16 = 0.05 * jax.random.normal(jax.random.fold_in(_tk, 500 + 16), (1250, 32), jnp.float32)
        tbl_17 = 0.05 * jax.random.normal(jax.random.fold_in(_tk, 500 + 17), (1250, 32), jnp.float32)
        tbl_18 = 0.05 * jax.random.normal(jax.random.fold_in(_tk, 500 + 18), (125000, 32), jnp.float32)
        tbl_19 = 0.05 * jax.random.normal(jax.random.fold_in(_tk, 500 + 19), (125000, 32), jnp.float32)
        tbl_20 = 0.05 * jax.random.normal(jax.random.fold_in(_tk, 500 + 20), (1250, 32), jnp.float32)
        tbl_21 = 0.05 * jax.random.normal(jax.random.fold_in(_tk, 500 + 21), (12500, 32), jnp.float32)
        tbl_22 = 0.05 * jax.random.normal(jax.random.fold_in(_tk, 500 + 22), (12500, 32), jnp.float32)
        tbl_23 = 0.05 * jax.random.normal(jax.random.fold_in(_tk, 500 + 23), (1250, 32), jnp.float32)
        tbl_24 = 0.05 * jax.random.normal(jax.random.fold_in(_tk, 500 + 24), (1250, 32), jnp.float32)
        tbl_25 = 0.05 * jax.random.normal(jax.random.fold_in(_tk, 500 + 25), (1250, 32), jnp.float32)
        _rk = jax.random.fold_in(_tk, 7)
        W_top1 = 0.0606339 * jax.random.normal(jax.random.fold_in(_tk, 801), (272, 512), jnp.float32)
        W_top2 = 0.0441942 * jax.random.normal(jax.random.fold_in(_tk, 802), (512, 256), jnp.float32)
        W_top3 = 0.0625 * jax.random.normal(jax.random.fold_in(_tk, 803), (256, 1), jnp.float32)
        b_top1 = jnp.zeros((512,), jnp.float32)
        b_top2 = jnp.zeros((256,), jnp.float32)
        return (dense_ctx, ids, tbl_0, tbl_1, tbl_2, tbl_3, tbl_4, tbl_5, tbl_6, tbl_7, tbl_8, tbl_9, tbl_10, tbl_11, tbl_12, tbl_13, tbl_14, tbl_15, tbl_16, tbl_17, tbl_18, tbl_19, tbl_20, tbl_21, tbl_22, tbl_23, tbl_24, tbl_25, W_top1, b_top1, W_top2, b_top2, W_top3)
    dense_ctx, ids, tbl_0, tbl_1, tbl_2, tbl_3, tbl_4, tbl_5, tbl_6, tbl_7, tbl_8, tbl_9, tbl_10, tbl_11, tbl_12, tbl_13, tbl_14, tbl_15, tbl_16, tbl_17, tbl_18, tbl_19, tbl_20, tbl_21, tbl_22, tbl_23, tbl_24, tbl_25, W_top1, b_top1, W_top2, b_top2, W_top3 = _rec_inputs()

    def _L0_rec_setup():
        import jax, jax.numpy as jnp
        import numpy as np
        M_FIELDS = 26
        H1 = 128
        H2 = 128
        BATCH = 256
        EMB_K = 32

        def _cin_layer(x_prev, x0, W, b):
            return jnp.einsum('bik,bjk,hij->bhk', x_prev, x0, W) + b[None, :, None]
        key = jax.random.key(seed)
        k0, k1, k2, k3, k4 = jax.random.split(key, 5)
        inputs = jax.random.normal(k0, (BATCH, M_FIELDS, EMB_K), dtype=jnp.float32)
        W1 = jax.random.normal(k1, (H1, M_FIELDS, M_FIELDS), dtype=jnp.float32) * 0.05
        b1 = jax.random.normal(k2, (H1,), dtype=jnp.float32) * 0.05
        W2 = jax.random.normal(k3, (H2, H1, M_FIELDS), dtype=jnp.float32) * 0.05
        b2 = jax.random.normal(k4, (H2,), dtype=jnp.float32) * 0.05
        return {'inputs': inputs, 'W1': W1, 'b1': b1, 'W2': W2, 'b2': b2}
    _L0_rec_all = _L0_rec_setup()
    _L0_rec_in = {k: v for k, v in _L0_rec_all.items() if k in ('W1', 'b1', 'W2', 'b2')}
    del _L0_rec_all
    return {'dense_ctx': dense_ctx, 'ids': ids, 'tbl_0': tbl_0, 'tbl_1': tbl_1, 'tbl_2': tbl_2, 'tbl_3': tbl_3, 'tbl_4': tbl_4, 'tbl_5': tbl_5, 'tbl_6': tbl_6, 'tbl_7': tbl_7, 'tbl_8': tbl_8, 'tbl_9': tbl_9, 'tbl_10': tbl_10, 'tbl_11': tbl_11, 'tbl_12': tbl_12, 'tbl_13': tbl_13, 'tbl_14': tbl_14, 'tbl_15': tbl_15, 'tbl_16': tbl_16, 'tbl_17': tbl_17, 'tbl_18': tbl_18, 'tbl_19': tbl_19, 'tbl_20': tbl_20, 'tbl_21': tbl_21, 'tbl_22': tbl_22, 'tbl_23': tbl_23, 'tbl_24': tbl_24, 'tbl_25': tbl_25, 'W_top1': W_top1, 'b_top1': b_top1, 'W_top2': W_top2, 'b_top2': b_top2, 'W_top3': W_top3, 'L0_rec_W1': _L0_rec_in['W1'], 'L0_rec_b1': _L0_rec_in['b1'], 'L0_rec_W2': _L0_rec_in['W2'], 'L0_rec_b2': _L0_rec_in['b2']}

def reference(dense_ctx, ids, tbl_0, tbl_1, tbl_2, tbl_3, tbl_4, tbl_5, tbl_6, tbl_7, tbl_8, tbl_9, tbl_10, tbl_11, tbl_12, tbl_13, tbl_14, tbl_15, tbl_16, tbl_17, tbl_18, tbl_19, tbl_20, tbl_21, tbl_22, tbl_23, tbl_24, tbl_25, W_top1, b_top1, W_top2, b_top2, W_top3, L0_rec_W1, L0_rec_b1, L0_rec_W2, L0_rec_b2):
    import jax
    import jax.numpy as jnp

    def _L0_rec_ref(inputs, W1, b1, W2, b2):
        import jax, jax.numpy as jnp
        import numpy as np
        M_FIELDS = 26
        H1 = 128
        H2 = 128
        BATCH = 256
        EMB_K = 32

        def _cin_layer(x_prev, x0, W, b):
            return jnp.einsum('bik,bjk,hij->bhk', x_prev, x0, W) + b[None, :, None]
        x1 = _cin_layer(inputs, inputs, W1, b1)
        x2 = _cin_layer(x1, inputs, W2, b2)
        res = jnp.concatenate([x1, x2], axis=1)
        return jnp.sum(res, axis=-1)
    e = jnp.stack([tbl_0[ids[:, 0]], tbl_1[ids[:, 1]], tbl_2[ids[:, 2]], tbl_3[ids[:, 3]], tbl_4[ids[:, 4]], tbl_5[ids[:, 5]], tbl_6[ids[:, 6]], tbl_7[ids[:, 7]], tbl_8[ids[:, 8]], tbl_9[ids[:, 9]], tbl_10[ids[:, 10]], tbl_11[ids[:, 11]], tbl_12[ids[:, 12]], tbl_13[ids[:, 13]], tbl_14[ids[:, 14]], tbl_15[ids[:, 15]], tbl_16[ids[:, 16]], tbl_17[ids[:, 17]], tbl_18[ids[:, 18]], tbl_19[ids[:, 19]], tbl_20[ids[:, 20]], tbl_21[ids[:, 21]], tbl_22[ids[:, 22]], tbl_23[ids[:, 23]], tbl_24[ids[:, 24]], tbl_25[ids[:, 25]]], axis=1)
    z = _L0_rec_ref(e, L0_rec_W1, L0_rec_b1, L0_rec_W2, L0_rec_b2)
    z = z.reshape(z.shape[0], -1)
    h = jnp.concatenate([z, dense_ctx], axis=1)
    h = jnp.maximum(h @ W_top1 + b_top1, 0.0)
    h = jnp.maximum(h @ W_top2 + b_top2, 0.0)
    y = h @ W_top3
    return y

_drawn_inputs = setup_inputs


def setup_inputs(seed=0):
    import zlib

    import numpy as np

    out = dict(_drawn_inputs(seed))
    spreads = {'b_top1': (0.0, 2.0), 'b_top2': (0.0, 0.8)}
    factors = {'tbl_0': 8.0,
     'tbl_1': 8.0,
     'tbl_2': 8.0,
     'tbl_3': 8.0,
     'tbl_4': 8.0,
     'tbl_5': 8.0,
     'tbl_6': 8.0,
     'tbl_7': 8.0,
     'tbl_8': 8.0,
     'tbl_9': 8.0,
     'tbl_10': 8.0,
     'tbl_11': 8.0,
     'tbl_12': 8.0,
     'tbl_13': 8.0,
     'tbl_14': 8.0,
     'tbl_15': 8.0,
     'tbl_16': 8.0,
     'tbl_17': 8.0,
     'tbl_18': 8.0,
     'tbl_19': 8.0,
     'tbl_20': 8.0,
     'tbl_21': 7.691,
     'tbl_22': 8.0,
     'tbl_23': 8.0,
     'tbl_24': 8.0,
     'tbl_25': 8.0,
     'L0_rec_W1': 7.915,
     'L0_rec_W2': 4.072,
     'dense_ctx': 5.96}
    for name, (base, spread) in spreads.items():
        noise = np.random.default_rng([zlib.crc32(name.encode()), seed]).standard_normal(out[name].shape)
        drawn = base * np.exp(spread * noise) if base else spread * noise
        out[name] = jnp.asarray(drawn.astype(out[name].dtype))
    for name, factor in factors.items():
        out[name] = (out[name] * factor).astype(out[name].dtype)
    return out
```

```python
from contextlib import ExitStack

import concourse.bass as bass
from concourse import mybir

P = 128
BATCH, FIELDS, DIM = 2048, 26, 32
TILES = BATCH // P
QUADS = P // DIM
DENSE, HID1, HID2 = 16, 512, 256
M1, M2 = HID1 // P, HID2 // P

HALF = FIELDS // 2
G1 = (HALF + 1) // 2
G2 = HALF - G1
GROUP_OF = [(0, G1), (G1, HALF)]
WITHIN = G1 * (G1 + 1) // 2 + G2 * (G2 + 1) // 2
ACROSS = G1 * G2

ROWS = [WITHIN + ACROSS + 1 + HALF, P // 2 + WITHIN]
W_AT = [0, P // 2]
X_AT = [WITHIN, 0]
ONE_AT = [WITHIN + ACROSS, ACROSS]
E_AT = WITHIN + ACROSS + 1
BASE = [0, ROWS[0]]
PAIRS = ROWS[0] + ROWS[1]

COLS = FIELDS + 1
C_ONE, C_B = HALF, HALF + 1
S_0, S_1, S_OWN = 0, HALF + 1, 2 * (HALF + 1)
NSLOT = S_OWN + HALF
SLOT_ONE = [S_0, S_1 + HALF]
OWN_ROWS = P // 2 + WITHIN

HR = DIM // 2
GR = 4
GROUPS = DIM // GR
GPH = GROUPS // 2

GX_D = [range(0, P // HALF), range(P // HALF, HALF)]
GX_ROWS = [len(r) * HALF for r in GX_D]


def within_row(q):
    if q < G1:
        return q * (q + 1) // 2, 0
    return G1 * (G1 + 1) // 2 + (q - G1) * (q - G1 + 1) // 2, G1


def wait(engine, sem, count):
    if not isinstance(count, int) or count > 0:
        engine.wait_ge(sem, count)


def build(nc, dense, ids, tables, w_top1, b_top1, w_top2, b_top2, w_top3, w1, b1, w2, b2, out):
    f32, i32 = mybir.dt.float32, mybir.dt.int32
    ALU, ACT = mybir.AluOpType, mybir.ActivationFunctionType
    ctx = ExitStack()
    with ctx:
        def sb(name, shape, dt=f32):
            return ctx.enter_context(nc.sbuf_tensor(name, shape, dt))

        def pb(name, shape):
            return ctx.enter_context(nc.psum_tensor(name, shape, f32))

        def sem(name):
            return ctx.enter_context(nc.semaphore(name))

        ids_all = sb("ids_all", [P, TILES, FIELDS], i32)
        idx = [sb(f"idx{p}", [P, FIELDS], i32) for p in range(2)]
        gathered = [sb(f"gathered{p}", [P, FIELDS * DIM]) for p in range(2)]
        et = [sb(f"et{p}", [P, DIM, FIELDS]) for p in range(2)]
        bd = [sb(f"bd{p}", [P, DIM, QUADS, COLS]) for p in range(2)]
        prod_mem = sb("prod_mem", [P, 2 * HR * PAIRS])
        prod = [prod_mem[:, h * HR * PAIRS:(h + 1) * HR * PAIRS].rearrange("p (r c) -> p r c", c=PAIRS)
                for h in range(2)]
        tt = [sb(f"tt{p}", [P, NSLOT, P]) for p in range(2)]
        gx = [sb(f"gx{p}", [P, 2, P]) for p in range(2)]
        cw = sb("cw", [P, 3 * HALF, P])
        w1t = sb("w1t", [P, 2, P])
        wgx = sb("wgx", [P, 2, P])
        z = sb("z", [P, 2, P])
        h1 = sb("h1", [P, M1, P])
        h2 = sb("h2", [P, M2, P])
        y = sb("y", [1, BATCH])
        dense_t = sb("dense_t", [DENSE, BATCH])
        wt1 = sb("wt1", [P, 2, HID1])
        wt1d = sb("wt1d", [DENSE, HID1])
        wt2 = sb("wt2", [P, M1, HID2])
        wt3 = sb("wt3", [P, M2])
        bt1 = sb("bt1", [P, M1])
        bt2 = sb("bt2", [P, M2])
        ident = sb("ident", [P, P])
        b1c = sb("b1c", [P, 1])
        b2c = sb("b2c", [P, 1])
        b2k = sb("b2k", [P, 1])
        w2t = sb("w2t", [P, FIELDS, P])
        w1r = sb("w1r", [P, FIELDS, FIELDS])
        w1q = sb("w1q", [P, FIELDS, FIELDS])
        w1z = sb("w1z", [P, PAIRS])
        w1p = sb("w1p", [P, PAIRS])
        w1x = sb("w1x", [P, HALF * HALF])
        cb = [sb(f"cb{n}", [P, HALF, ROWS[n]]) for n in range(2)]
        cb_own = sb("cb_own", [P, HALF, OWN_ROWS])
        H3, G21 = HALF ** 3, G1 * G1 * G2 + G2 * G2 * G1
        fold_half = [prod_mem[:, n * H3:(n + 1) * H3].rearrange("p (x y d) -> p x y d", x=HALF, y=HALF)
                     for n in range(2)]
        fold_group = [[None, None], [None, None]]
        for n in range(2):
            at = 2 * H3 + n * G21
            for g, (size, other) in enumerate(((G1, G2), (G2, G1))):
                fold_group[n][g] = prod_mem[:, at:at + size * size * other].rearrange(
                    "p (x y d) -> p x y d", x=size, y=size)
                at += size * size * other
        w2r = bd[1][:, :, :, :].rearrange("p r q s -> p (r q s)")[:, 0:P * FIELDS].rearrange(
            "p (i d) -> p i d", d=FIELDS)
        dense_n = gathered[1][:, 0:TILES * DENSE].rearrange("p (t f) -> p t f", f=DENSE)

        ps_t = [[pb(f"ps_t{b}{n}", [P, 512]) for n in range(2)] for b in range(2)]
        ps_z = pb("ps_z", [P, 512])
        ps_1 = pb("ps_1", [P, 512])
        ps_2 = pb("ps_2", [P, 512])
        ps_s = pb("ps_s", [P, 512])
        z1_ps, z2_ps = ps_z[:, 0:P], ps_z[:, P:2 * P]
        y_ps = ps_2[0:1, M2 * P:(M2 + 1) * P]

        s_ids = sem("s_ids")
        s_w2 = sem("s_w2")
        s_w1 = sem("s_w1")
        s_dense = sem("s_dense")
        s_top = sem("s_top")
        s_ident0 = sem("s_ident0")
        s_ident = sem("s_ident")
        s_const = sem("s_const")
        s_w1s = sem("s_w1s")
        s_w1p = sem("s_w1p")
        s_prep_ps = sem("s_prep_ps")
        s_prep_ev = sem("s_prep_ev")
        s_fold_ps = sem("s_fold_ps")
        s_fold_ev = sem("s_fold_ev")
        s_fold = sem("s_fold")
        s_zero = sem("s_zero")
        s_prodc = sem("s_prodc")
        s_b2 = sem("s_b2")
        idx_ready = [sem(f"idx_ready{p}") for p in range(2)]
        tile_begun = sem("tile_begun")
        gather_done = [sem(f"gather_done{p}") for p in range(2)]
        et_ready = [sem(f"et_ready{p}") for p in range(2)]
        bd_ready = [sem(f"bd_ready{p}") for p in range(2)]
        prod_ready = [sem(f"prod_ready{h}") for h in range(2)]
        half_done = [sem(f"half_done{h}") for h in range(2)]
        group_done = [sem(f"group_done{b}") for b in range(2)]
        t_copied = [sem(f"t_copied{b}") for b in range(2)]
        gx_ready = [sem(f"gx_ready{p}") for p in range(2)]
        z_done = [sem(f"z_done{p}") for p in range(2)]
        z_ready = sem("z_ready")
        top1_done = sem("top1_done")
        h1_ready = sem("h1_ready")
        top2_done = sem("top2_done")
        h2_ready = sem("h2_ready")
        y_done = sem("y_done")
        y_ready = sem("y_ready")
        s_out = sem("s_out")

        GATHERED = 16 * FIELDS
        MOVED = 16 * HALF
        prep_bank = [ps_z, ps_1, ps_2, ps_s]
        fold_bank = [ps_t[0][0], ps_t[0][1], ps_t[1][0], ps_t[1][1]]

        DENSE_TURNS = [range(t, t + 4) for t in range(0, TILES, 4)]
        W2_TURNS = [range(d, min(d + 4, FIELDS)) for d in range(0, FIELDS, 4)]
        pieces = [(cb[0], d, ROWS[0], S_0 + 1 + d) for d in range(HALF)]
        pieces += [(cb[1], d, ROWS[1], S_1 + d) for d in range(HALF)]
        pieces += [(cb_own, d, OWN_ROWS, S_OWN + d) for d in range(HALF)]
        CW_TURNS = [range(i, min(i + 4, len(pieces))) for i in range(0, len(pieces), 4)]
        FIRST_W2 = len(DENSE_TURNS)
        FIRST_BASE = FIRST_W2 + len(W2_TURNS)
        Z1_TURN = FIRST_BASE + FIELDS
        FIRST_CW = Z1_TURN + 1
        PREP = FIRST_CW + len(CW_TURNS)
        OWN_COL = P
        z1_pieces = [(w1z[:, BASE[n]:BASE[n] + ROWS[n]], ROWS[n], w1t[0:ROWS[n], n, :]) for n in range(2)]
        z1_pieces += [(w1x[:, GX_D[m][0] * HALF:(GX_D[m][-1] + 1) * HALF], GX_ROWS[m], wgx[0:GX_ROWS[m], m, :])
                      for m in range(2)]

        block = ctx.enter_context(nc.Block())

        @block.sync
        def _(sp):
            sp.dma_start(ids_all[:, :, :], ids.rearrange("(t p) f -> p t f", p=P)).then_inc(s_ids, 16)
            sp.dma_start(w1r[:, :, :], w1).then_inc(s_w1, 16)
            sp.dma_start(b1c[:, :], b1.rearrange("(p a) -> p a", a=1)).then_inc(s_w1, 16)
            sp.dma_start(w2r, w2).then_inc(s_w2, 16)

            def move_gx(k, p):
                for b in range(2):
                    sp.wait_ge(t_copied[b], 8 * k + 4 * p + 4)
                wait(sp, z_done[p], k)
                for m in range(2):
                    for j, d in enumerate(GX_D[m]):
                        sp.dma_start(gx[p][j * HALF:(j + 1) * HALF, m, :],
                                     tt[p][E_AT:E_AT + HALF, S_0 + 1 + d, :]).then_inc(gx_ready[p], 16)

            for p in range(2):
                move_gx(0, p)
            with nc.sync.Fori(1, TILES // 2) as k:
                for p in range(2):
                    move_gx(k, p)
            sp.wait_ge(y_ready, TILES)
            sp.dma_start(out.rearrange("b a -> a b"), y[:, :]).then_inc(s_out, 16)
            sp.wait_ge(s_out, 16)

        @block.gpsimd
        def _(pool):
            nc.gpsimd.memset(ident[:, :], 0.0).then_inc(s_ident0, 1)
            pool.wait_ge(s_ident0, 1)
            nc.gpsimd.affine_select(out=ident[:, :], in_=ident[:, :], compare_op=ALU.not_equal, fill=1.0, base=0,
                                    pattern=[[-1, P]], channel_multiplier=1).then_inc(s_ident, 1)

            def gather(p):
                for f in range(FIELDS):
                    pool.indirect_dma_start(
                        out=gathered[p][:, f * DIM:(f + 1) * DIM], out_offset=None, in_=tables[f],
                        in_offset=bass.IndirectOffsetOnAxis(ap=idx[p][:, f:f + 1], axis=0),
                    ).then_inc(gather_done[p], 16)

            for p in range(2):
                pool.wait_ge(idx_ready[p], 1)
                if p == 1:
                    pool.wait_ge(s_prep_ps, FIRST_W2)
                gather(p)
            with nc.gpsimd.Fori(1, TILES // 2) as k:
                for p in range(2):
                    pool.wait_ge(idx_ready[p], k + 1)
                    pool.wait_ge(et_ready[p], k)
                    nc.gpsimd.sem_inc(tile_begun, 1)
                    gather(p)

        @block.vector
        def _(dve):
            def next_indices(t, p):
                nc.vector.tensor_copy(idx[p][:, :], ids_all[:, bass.ds(t, 1), :].rearrange("p a f -> p (a f)")
                                      ).then_inc(idx_ready[p], 1)

            dve.wait_ge(s_ids, 16)
            next_indices(0, 0)
            next_indices(1, 1)

            def diagonal_init(p):
                nc.vector.memset(bd[p][:, :, :, :], 0.0).then_inc(s_const, 1)
                dve.wait_ge(s_const, 1 + 2 * p)
                for q in range(QUADS):
                    last = nc.vector.memset(bd[p][q * DIM:(q + 1) * DIM, :, q, C_ONE:C_ONE + 1], 1.0)
                last.then_inc(s_const, 1)

            nc.vector.memset(w1z[:, :], 0.0).then_inc(s_w1s, 1)
            dve.wait_ge(s_w1, 32)
            nc.vector.tensor_tensor(w1q[:, :, :], w1r[:, :, :], w1r[:, :, :].rearrange("p x y -> p y x"),
                                    ALU.add).then_inc(s_w1s, 1)
            dve.wait_ge(s_w1s, 2)
            diag = slice(0, FIELDS * FIELDS, FIELDS + 1)
            nc.vector.tensor_copy(w1q[:, :, :].rearrange("p x y -> p (x y)")[:, diag],
                                  w1r[:, :, :].rearrange("p x y -> p (x y)")[:, diag]).then_inc(s_w1s, 1)
            dve.wait_ge(s_w1s, 3)
            for n in range(2):
                f0 = n * HALF
                for q in range(HALF):
                    row, p0 = within_row(q)
                    at = BASE[n] + W_AT[n] + row
                    nc.vector.tensor_copy(w1z[:, at:at + q - p0 + 1], w1q[:, f0 + q, f0 + p0:f0 + q + 1])
                at = BASE[n] + X_AT[n]
                nc.vector.tensor_copy(w1z[:, at:at + ACROSS].rearrange("p (y x) -> p y x", x=G1),
                                      w1q[:, f0 + G1:f0 + HALF, f0:f0 + G1])
            nc.vector.tensor_copy(w1x[:, :].rearrange("p (d a) -> p d a", a=HALF), w1q[:, HALF:, 0:HALF])
            nc.vector.tensor_copy(w1z[:, ONE_AT[0]:ONE_AT[0] + 1], b1c[:, :]).then_inc(s_w1s, 1)
            dve.wait_ge(s_w1s, 4)
            nc.vector.tensor_copy(w1p[:, :], w1z[:, :]).then_inc(s_w1s, 1)
            dve.wait_ge(s_w1s, 5)
            at = BASE[1] + ONE_AT[1]
            nc.vector.tensor_copy(w1p[:, at:at + 1], b1c[:, :]).then_inc(s_w1p, 1)
            diagonal_init(0)
            nc.vector.memset(cb_own[:, :, WITHIN:P // 2], 0.0)
            for p in range(2):
                last = nc.vector.memset(tt[p][P // 4:P // 2, S_OWN:, :], 0.0)
            last.then_inc(s_zero, 1)
            dve.wait_ge(s_prep_ps, FIRST_BASE)
            diagonal_init(1)

            for x in range(FIELDS):
                n, q = x // HALF, x % HALF
                g = int(q >= G1)
                bank = fold_bank[x % 4]
                size, other = (G1, G2) if g == 0 else (G2, G1)
                dve.wait_ge(s_fold_ps, x + 1)
                nc.vector.tensor_copy(fold_half[n][:, q, :, :],
                                      bank[:, 0:HALF * HALF].rearrange("p (y d) -> p y d", d=HALF))
                nc.vector.tensor_copy(fold_group[n][g][:, q - GROUP_OF[g][0], :, :],
                                      bank[:, HALF * HALF:HALF * HALF + size * other].rearrange(
                                          "p (y d) -> p y d", d=other)).then_inc(s_fold_ev, 1)

            dve.wait_ge(s_fold_ev, FIELDS)
            dve.wait_ge(s_prep_ev, FIRST_BASE + FIELDS)
            for second in range(2):
                if second:
                    dve.wait_ge(s_fold, 1)
                for n in range(2):
                    for q in range(HALF):
                        row, p0 = within_row(q)
                        g = int(q >= G1)
                        count = q - p0 + 1 - second
                        if not count:
                            continue
                        o = cb[n][:, :, W_AT[n] + row:W_AT[n] + row + count]
                        o_own = cb_own[:, GROUP_OF[1 - g][0]:GROUP_OF[1 - g][1], W_AT[n] + row:W_AT[n] + row + count]
                        fh, fg = fold_half[n], fold_group[n][g]
                        if second:
                            term = fh[:, q, p0:q, :].rearrange("p y d -> p d y")
                            term_own = fg[:, q - p0, 0:q - p0, :].rearrange("p y d -> p d y")
                        else:
                            term = fh[:, p0:q + 1, q, :].rearrange("p x d -> p d x")
                            term_own = fg[:, 0:q - p0 + 1, q - p0, :].rearrange("p x d -> p d x")
                        nc.vector.tensor_tensor(o, o, term, ALU.add)
                        nc.vector.tensor_tensor(o_own, o_own, term_own, ALU.add)
                    o = cb[n][:, :, X_AT[n]:X_AT[n] + ACROSS].rearrange("p d (y x) -> p d y x", x=G1)
                    if second:
                        term = fold_half[n][:, G1:, 0:G1, :].rearrange("p x y d -> p d x y")
                    else:
                        term = fold_half[n][:, 0:G1, G1:, :].rearrange("p x y d -> p d y x")
                    last = nc.vector.tensor_tensor(o, o, term, ALU.add)
                last.then_inc(s_fold, 1)
            dve.wait_ge(s_fold, 2)
            for h in range(2):
                for n in range(2):
                    at = BASE[n] + ONE_AT[n]
                    nc.vector.memset(prod[h][:, :, at:at + 1], 1.0)
                last = nc.vector.memset(prod[h][:, :, BASE[1] + ACROSS + 1:BASE[1] + W_AT[1]], 0.0)
            last.then_inc(s_prodc, 1)

            def tile(k, p):
                t = 2 * k + p
                dve.wait_ge(gather_done[p], GATHERED * (k + 1))
                wait(dve, bd_ready[p], 2 * k)
                wait(dve, prod_ready[1], t)
                nc.vector.transpose(et[p][:, :, :].rearrange("p r f -> p f r"),
                                    gathered[p][:, :].rearrange("p (f k) -> p f k", k=DIM)).then_inc(et_ready[p], 1)
                if not isinstance(k, int) or k < TILES // 2 - 1:
                    next_indices(t + 2, p)
                dve.wait_ge(et_ready[p], k + 1)
                for h in range(2):
                    wait(dve, half_done[h], t)
                    e = et[p][:, h * HR:(h + 1) * HR, :]
                    for n in range(2):
                        f0 = n * HALF
                        for q in range(HALF):
                            row, p0 = within_row(q)
                            at, count = BASE[n] + W_AT[n] + row, q - p0 + 1
                            nc.vector.tensor_tensor(
                                prod[h][:, :, at:at + count], e[:, :, f0 + p0:f0 + q + 1],
                                e[:, :, f0 + q:f0 + q + 1].broadcast_to([P, HR, count]), ALU.mult)
                        at = BASE[n] + X_AT[n]
                        nc.vector.tensor_tensor(
                            prod[h][:, :, at:at + ACROSS].rearrange("p r (y x) -> p r y x", x=G1),
                            e[:, :, f0:f0 + G1].unsqueeze(2).broadcast_to([P, HR, G2, G1]),
                            e[:, :, f0 + G1:f0 + HALF].unsqueeze(3).broadcast_to([P, HR, G2, G1]), ALU.mult)
                    nc.vector.tensor_copy(prod[h][:, :, E_AT:E_AT + HALF], e[:, :, 0:HALF]).then_inc(prod_ready[h], 1)

            for p in range(2):
                tile(0, p)
            with nc.vector.Fori(1, TILES // 2 - 1) as k:
                for p in range(2):
                    tile(k, p)
            for p in range(2):
                tile(TILES // 2 - 1, p)

        @block.scalar
        def _(act):
            act.dma_start(dense_n, dense.rearrange("(t p) f -> p t f", p=P)).then_inc(s_dense, 16)
            act.dma_start(wt1[:, :, :], w_top1[0:2 * P, :].rearrange("(c p) n -> p c n", p=P)).then_inc(s_top, 16)
            act.dma_start(wt1d[:, :], w_top1[2 * P:, :]).then_inc(s_top, 16)
            act.dma_start(wt2[:, :, :], w_top2.rearrange("(c p) n -> p c n", p=P)).then_inc(s_top, 16)
            with nc.allow_non_contiguous_dma(reason="a few hundred biases, once"):
                act.dma_start(wt3[:, :], w_top3.rearrange("(c p) a -> p (c a)", p=P)).then_inc(s_top, 16)
                act.dma_start(bt1[:, :], b_top1.rearrange("(c p) -> p c", p=P)).then_inc(s_top, 16)
                act.dma_start(bt2[:, :], b_top2.rearrange("(c p) -> p c", p=P)).then_inc(s_top, 16)
            act.dma_start(b2c[:, :], b2.rearrange("(p a) -> p a", a=1)).then_inc(s_top, 16)

            def copy(dst, src):
                return nc.scalar.activation(dst, src, ACT.Copy)

            for i, ts in enumerate(DENSE_TURNS):
                act.wait_ge(s_prep_ps, i + 1)
                copy(dense_t[:, ts[0] * P:(ts[-1] + 1) * P],
                     prep_bank[i % 4][0:DENSE, 0:len(ts) * P]).then_inc(s_prep_ev, 1)
            for i, ds in enumerate(W2_TURNS):
                turn = FIRST_W2 + i
                act.wait_ge(s_prep_ps, turn + 1)
                copy(w2t[:, ds[0]:ds[-1] + 1, :].rearrange("p d h -> p (d h)"),
                     prep_bank[turn % 4][:, 0:len(ds) * P]).then_inc(s_prep_ev, 1)
            for d in range(FIELDS):
                turn = FIRST_BASE + d
                own, q = d // HALF, d % HALF
                n = 1 - own
                act.wait_ge(s_prep_ps, turn + 1)
                copy(cb[n][:, q, :], prep_bank[turn % 4][:, 0:ROWS[n]])
                copy(cb_own[:, q, W_AT[own]:W_AT[own] + WITHIN],
                     prep_bank[turn % 4][:, OWN_COL:OWN_COL + WITHIN]).then_inc(s_prep_ev, 1)
            act.wait_ge(s_prep_ps, Z1_TURN + 1)
            for j, (_, rows, dst) in enumerate(z1_pieces):
                last = copy(dst, prep_bank[Z1_TURN % 4][0:rows, j * P:(j + 1) * P])
            last.then_inc(s_prep_ev, 1)
            act.wait_ge(s_top, 16 * 7)
            nc.scalar.mul(b2k[:, :], b2c[:, :], float(DIM)).then_inc(s_b2, 1)

            def fields_out(k, p):
                act.wait_ge(et_ready[p], k + 1)
                wait(act, half_done[1], 2 * k + p)
                for h in range(2):
                    rs = slice(h * HR, (h + 1) * HR)
                    for q in range(QUADS):
                        rows = slice(q * DIM, (q + 1) * DIM)
                        for f0, c0 in ((0, 0), (HALF, C_B)):
                            last = copy(bd[p][rows, rs, q, c0:c0 + HALF], et[p][rows, rs, f0:f0 + HALF])
                    last.then_inc(bd_ready[p], 1)

            def triples_out(k, p):
                wait(act, z_done[p], k)
                wait(act, gx_ready[p], MOVED * k)
                for g in range(GROUPS):
                    b = g % 2
                    if g % GPH == GPH - 1:
                        act.wait_ge(half_done[g // GPH], 2 * k + p + 1)
                    elif b:
                        act.wait_ge(group_done[1], 4 * k + 2 * p + g // GPH + 1)
                    else:
                        act.wait_ge(group_done[0], 8 * k + 4 * p + g // 2 + 1)
                    samples = slice(g * GR, (g + 1) * GR)
                    own = [(n, slice(W_AT[n], W_AT[n] + WITHIN), S_OWN, n * C_B, HALF) for n in range(2)]
                    for n, rows, s0, c0, count in (
                            (0, slice(0, ROWS[0]), S_0, C_ONE, HALF + 1), (1, slice(0, ROWS[1]), S_1, 0, HALF + 1), *own):
                        last = copy(
                            tt[p][rows, s0:s0 + count, :].rearrange("p s (q r) -> p s q r", q=QUADS)[:, :, :, samples],
                            ps_t[b][n][rows, 0:GR * QUADS * COLS].rearrange(
                                "p (r q s) -> p s q r", q=QUADS, s=COLS)[:, c0:c0 + count, :, :])
                    last.then_inc(t_copied[b], 1)

            def z_out(k, p):
                act.wait_ge(z_done[p], k + 1)
                wait(act, top1_done, 2 * k + p)
                copy(z[:, 0, :], z1_ps)
                nc.scalar.activation(z[:, 1, :], z2_ps, ACT.Identity, bias=b2k[:, 0:1]).then_inc(z_ready, 1)

            def mlp_out(t):
                act.wait_ge(top1_done, t + 1)
                wait(act, top2_done, t)
                for m in range(M1):
                    last = nc.scalar.activation(h1[:, m, :], ps_1[:, m * P:(m + 1) * P], ACT.Relu,
                                                bias=bt1[:, m:m + 1])
                last.then_inc(h1_ready, 1)
                act.wait_ge(top2_done, t + 1)
                wait(act, y_done, t)
                for m in range(M2):
                    last = nc.scalar.activation(h2[:, m, :], ps_2[:, m * P:(m + 1) * P], ACT.Relu,
                                                bias=bt2[:, m:m + 1])
                last.then_inc(h2_ready, 1)
                act.wait_ge(y_done, t + 1)
                copy(y[:, bass.ds(t * P, P)], y_ps).then_inc(y_ready, 1)

            act.wait_ge(s_const, 4)
            fields_out(0, 0)
            act.wait_ge(s_fold_ev, FIELDS)
            act.wait_ge(s_zero, 1)
            act.wait_ge(s_b2, 1)
            triples_out(0, 0)
            for i, turn_pieces in enumerate(CW_TURNS):
                act.wait_ge(s_prep_ps, FIRST_CW + i + 1)
                bank = prep_bank[(FIRST_CW + i) % 4]
                runs = []
                for j, c in enumerate(turn_pieces):
                    if runs and pieces[runs[-1][0]][2] == pieces[c][2]:
                        runs[-1][2] += 1
                    else:
                        runs.append([c, j, 1])
                for c, j, count in runs:
                    rows = pieces[c][2]
                    last = copy(cw[0:rows, c:c + count, :].rearrange("p s h -> p (s h)"),
                                bank[0:rows, j * P:(j + count) * P])
                last.then_inc(s_prep_ev, 1)
            fields_out(0, 1)
            z_out(0, 0)

            def tile(k, p, t):
                triples_out(k, p)
                mlp_out(t - 1)
                fields_out(k + p, 1 - p)
                z_out(k, p)

            tile(0, 1, 1)
            tile(1, 0, 2)
            with nc.scalar.Fori(1, TILES // 2 - 1) as k:
                tile(k, 1, 2 * k + 1)
                tile(k + 1, 0, 2 * k + 2)
            triples_out(TILES // 2 - 1, 1)
            mlp_out(TILES - 2)
            z_out(TILES // 2 - 1, 1)
            mlp_out(TILES - 1)

        @block.tensor
        def _(pe):
            def turn_free(turn):
                wait(pe, s_prep_ev, turn - 3)

            pe.wait_ge(s_ident, 1)
            pe.wait_ge(s_dense, 16)
            for i, ts in enumerate(DENSE_TURNS):
                turn_free(i)
                for j, t in enumerate(ts):
                    last = nc.tensor.transpose(prep_bank[i % 4][0:DENSE, j * P:(j + 1) * P], dense_n[:, t, :],
                                               ident[:, :])
                last.then_inc(s_prep_ps, 1)
            pe.wait_ge(s_w2, 16)
            for i, ds in enumerate(W2_TURNS):
                turn = FIRST_W2 + i
                turn_free(turn)
                for j, d in enumerate(ds):
                    last = nc.tensor.transpose(prep_bank[turn % 4][:, j * P:(j + 1) * P], w2r[:, :, d], ident[:, :])
                last.then_inc(s_prep_ps, 1)
            pe.wait_ge(s_w1p, 1)
            pe.wait_ge(s_prep_ev, FIRST_BASE)
            for d in range(FIELDS):
                turn = FIRST_BASE + d
                own, q = d // HALF, d % HALF
                n = 1 - own
                turn_free(turn)
                nc.tensor.matmul(prep_bank[turn % 4][:, 0:ROWS[n]], w2t[:, d, :], w1p[:, BASE[n]:BASE[n] + ROWS[n]],
                                 start=True, stop=True)
                at = BASE[own] + W_AT[own]
                nc.tensor.matmul(prep_bank[turn % 4][:, OWN_COL:OWN_COL + WITHIN], w2t[:, d, :],
                                 w1p[:, at:at + WITHIN], start=True, stop=True).then_inc(s_prep_ps, 1)
                g = int(q >= G1)
                y0, y1 = (own * HALF + v for v in GROUP_OF[g])
                d0, d1 = (own * HALF + v for v in GROUP_OF[1 - g])
                bank = fold_bank[d % 4]
                wait(pe, s_fold_ev, d - 3)
                nc.tensor.matmul(bank[:, 0:HALF * HALF].rearrange("p (y d) -> p y d", d=HALF), w2t[:, d, :],
                                 w1q[:, own * HALF:(own + 1) * HALF, n * HALF:(n + 1) * HALF], start=True, stop=True)
                nc.tensor.matmul(bank[:, HALF * HALF:HALF * HALF + ACROSS].rearrange("p (y d) -> p y d", d=d1 - d0),
                                 w2t[:, d, :], w1q[:, y0:y1, d0:d1], start=True, stop=True).then_inc(s_fold_ps, 1)
            turn_free(Z1_TURN)
            for j, (src, rows, _) in enumerate(z1_pieces):
                last = nc.tensor.transpose(prep_bank[Z1_TURN % 4][0:rows, j * P:(j + 1) * P], src, ident[:, :])
            last.then_inc(s_prep_ps, 1)

            def triples(k, p):
                for g in range(GROUPS):
                    h, b = g // GPH, g % 2
                    if g % GPH == 0:
                        pe.wait_ge(bd_ready[p], 2 * k + h + 1)
                        pe.wait_ge(prod_ready[h], 2 * k + p + 1)
                    wait(pe, t_copied[b], 8 * k + 4 * p + g // 2)
                    for j in range(GR):
                        r = g * GR + j
                        for n in range(2):
                            last = nc.tensor.matmul(
                                ps_t[b][n][0:ROWS[n], j * QUADS * COLS:(j + 1) * QUADS * COLS],
                                prod[h][:, r - h * HR, BASE[n]:BASE[n] + ROWS[n]],
                                bd[p][:, r, :, :].rearrange("p q s -> p (q s)"), start=True, stop=True)
                    if g % GPH == GPH - 1:
                        last.then_inc(half_done[h], 1)
                    else:
                        last.then_inc(group_done[b], 1)

            N_PIECES = len(pieces)

            def z2_part(p, lo, hi):
                for i in range(lo, hi):
                    _, _, rows, s = pieces[i]
                    nc.tensor.matmul(z2_ps, cw[0:rows, i, :], tt[p][0:rows, s, :],
                                     start=(i == 0), stop=(i == N_PIECES - 1))

            def z_begin(k, p):
                for b in range(2):
                    pe.wait_ge(t_copied[b], 8 * k + 4 * p + 4)
                wait(pe, z_ready, 2 * k + p)

            def z1_part(k, p):
                for n in range(2):
                    nc.tensor.matmul(z1_ps, w1t[0:ROWS[n], n, :], tt[p][0:ROWS[n], SLOT_ONE[n], :],
                                     start=(n == 0), stop=False)
                pe.wait_ge(gx_ready[p], MOVED * (k + 1))
                for m in range(2):
                    last = nc.tensor.matmul(z1_ps, wgx[0:GX_ROWS[m], m, :], gx[p][0:GX_ROWS[m], m, :],
                                            start=False, stop=(m == 1))
                last.then_inc(z_done[p], 1)

            def top1(t):
                pe.wait_ge(z_ready, t + 1)
                wait(pe, h1_ready, t)
                for m in range(M1):
                    cols = slice(m * P, (m + 1) * P)
                    nc.tensor.matmul(ps_1[:, cols], wt1d[:, cols], dense_t[:, bass.ds(t * P, P)],
                                     start=True, stop=False)
                    nc.tensor.matmul(ps_1[:, cols], wt1[:, 0, cols], z[:, 0, :], start=False, stop=False)
                    last = nc.tensor.matmul(ps_1[:, cols], wt1[:, 1, cols], z[:, 1, :], start=False, stop=True)
                last.then_inc(top1_done, 1)

            def top2(t):
                pe.wait_ge(h1_ready, t + 1)
                wait(pe, h2_ready, t)
                wait(pe, y_ready, t)
                for m in range(M2):
                    for c in range(M1):
                        last = nc.tensor.matmul(ps_2[:, m * P:(m + 1) * P], wt2[:, c, m * P:(m + 1) * P], h1[:, c, :],
                                                start=(c == 0), stop=(c == M1 - 1))
                last.then_inc(top2_done, 1)

            def top3(t):
                pe.wait_ge(h2_ready, t + 1)
                for c in range(M2):
                    last = nc.tensor.matmul(y_ps, wt3[:, c:c + 1], h2[:, c, :], start=(c == 0), stop=(c == M2 - 1))
                last.then_inc(y_done, 1)

            def tile(k, p, t):
                triples(k, p)
                top1(t - 1)
                z_begin(k, p)
                z2_part(p, 0, N_PIECES // 2)
                top2(t - 1)
                z2_part(p, N_PIECES // 2, N_PIECES * 3 // 4)
                top3(t - 1)
                z2_part(p, N_PIECES * 3 // 4, N_PIECES)
                z1_part(k, p)

            pe.wait_ge(s_fold_ev, FIELDS)
            pe.wait_ge(s_prodc, 1)
            triples(0, 0)
            pe.wait_ge(s_fold, 2)
            for i, turn_pieces in enumerate(CW_TURNS):
                turn = FIRST_CW + i
                turn_free(turn)
                for j, c in enumerate(turn_pieces):
                    src, d, rows, _ = pieces[c]
                    last = nc.tensor.transpose(prep_bank[turn % 4][0:rows, j * P:(j + 1) * P], src[:, d, :],
                                               ident[:, :])
                last.then_inc(s_prep_ps, 1)
            pe.wait_ge(s_prep_ev, PREP)
            z_begin(0, 0)
            z2_part(0, 0, N_PIECES)
            z1_part(0, 0)
            pe.wait_ge(s_top, 16 * 7)
            tile(0, 1, 1)
            tile(1, 0, 2)
            with nc.tensor.Fori(1, TILES // 2 - 1) as k:
                tile(k, 1, 2 * k + 1)
                tile(k + 1, 0, 2 * k + 2)
            tile(TILES // 2 - 1, 1, TILES - 1)
            top1(TILES - 1)
            top2(TILES - 1)
            top3(TILES - 1)


TABLES = [f"tbl_{f}" for f in range(FIELDS)]
INPUTS = ["dense_ctx", "ids", *TABLES, "W_top1", "b_top1", "W_top2", "b_top2", "W_top3",
          "L0_rec_W1", "L0_rec_b1", "L0_rec_W2", "L0_rec_b2"]


def kernel(**inputs):
    import numpy as np
    import concourse.bacc as bacc
    from concourse import mybir
    from concourse.bass_utils import run_bass_kernel_spmd

    nc = bacc.Bacc("TRN2", target_bir_lowering=False, num_devices=1)
    arrays, ap = {}, {}
    for name in INPUTS:
        a = np.ascontiguousarray(inputs[name])
        arrays[f"in_{name}"] = a
        ap[name] = nc.dram_tensor(f"in_{name}", a.shape, mybir.dt.from_np(a.dtype), kind="ExternalInput").ap()
    out = nc.dram_tensor("out", (BATCH, 1), mybir.dt.float32, kind="ExternalOutput").ap()
    build(nc, ap["dense_ctx"], ap["ids"], [ap[t] for t in TABLES], ap["W_top1"], ap["b_top1"], ap["W_top2"],
          ap["b_top2"], ap["W_top3"], ap["L0_rec_W1"], ap["L0_rec_b1"], ap["L0_rec_W2"], ap["L0_rec_b2"], out)
    result = run_bass_kernel_spmd(nc, [arrays], core_ids=[0])
    return result.results[0]["out"]
```

```python
from contextlib import ExitStack

import concourse.bass as bass
from concourse import mybir

P = 128
BATCH, FIELDS, DIM = 2048, 26, 32
TILES = BATCH // P
QUADS = P // DIM
DENSE, HID1, HID2 = 16, 512, 256
M1, M2 = HID1 // P, HID2 // P

STACK = [(0, 0, 0), (DENSE, 1, 0), (2 * DENSE, 2, 0), (64, 0, 1), (64 + DENSE, 1, 1), (96, 0, 2)]
STACK_ROWS = 96 + DENSE

HALF = FIELDS // 2
G1 = (HALF + 1) // 2
G2 = HALF - G1
GROUP_OF = [(0, G1), (G1, HALF)]
WITHIN = G1 * (G1 + 1) // 2 + G2 * (G2 + 1) // 2
ACROSS = G1 * G2

ROWS = [WITHIN + ACROSS + 1 + HALF, P // 2 + WITHIN]
W_AT = [0, P // 2]
X_AT = [WITHIN, 0]
ONE_AT = [WITHIN + ACROSS, ACROSS]
E_AT = WITHIN + ACROSS + 1
BASE = [0, ROWS[0]]
PAIRS = ROWS[0] + ROWS[1]

COLS = FIELDS + 1
C_ONE, C_B = HALF, HALF + 1
S_0, S_1, S_OWN = 0, HALF + 1, 2 * (HALF + 1)
NSLOT = S_OWN + HALF
SLOT_ONE = [S_0, S_1 + HALF]
OWN_ROWS = P // 2 + WITHIN

AT_OWN = [ROWS[1], ROWS[0]]
AT_FH = [c + WITHIN for c in AT_OWN]
AT_FG = [c + HALF * HALF for c in AT_FH]
PACK = [c + ACROSS for c in AT_FG]

HR = DIM // 2
GR = 4
GROUPS = DIM // GR
GPH = GROUPS // 2

GX_D = [range(0, P // HALF), range(P // HALF, HALF)]
GX_ROWS = [len(r) * HALF for r in GX_D]


def within_row(q):
    if q < G1:
        return q * (q + 1) // 2, 0
    return G1 * (G1 + 1) // 2 + (q - G1) * (q - G1 + 1) // 2, G1


def wait(engine, sem, count):
    if not isinstance(count, int) or count > 0:
        engine.wait_ge(sem, count)


def build(nc, dense, ids, tables, w_top1, b_top1, w_top2, b_top2, w_top3, w1, b1, w2, b2, out):
    f32, bf16, i32 = mybir.dt.float32, mybir.dt.bfloat16, mybir.dt.int32
    ALU, ACT = mybir.AluOpType, mybir.ActivationFunctionType
    ctx = ExitStack()
    with ctx:
        def sb(name, shape, dt=f32):
            return ctx.enter_context(nc.sbuf_tensor(name, shape, dt))

        def pb(name, shape):
            return ctx.enter_context(nc.psum_tensor(name, shape, f32))

        def sem(name):
            return ctx.enter_context(nc.semaphore(name))

        ids_all = sb("ids_all", [P, TILES, FIELDS], i32)
        idx = [sb(f"idx{p}", [P, FIELDS], i32) for p in range(2)]
        gathered = [sb(f"gathered{p}", [P, FIELDS * DIM]) for p in range(2)]
        et = [sb(f"et{p}", [P, DIM, FIELDS]) for p in range(2)]
        bd = [sb(f"bd{p}", [P, DIM, QUADS, COLS]) for p in range(2)]
        prod = [sb(f"prod{h}", [P, HR, PAIRS]) for h in range(2)]
        tt = [sb(f"tt{p}", [P, NSLOT, P]) for p in range(2)]
        gx = [sb(f"gx{p}", [P, 2, P]) for p in range(2)]
        cw = sb("cw", [P, 3 * HALF, P])
        w1t = sb("w1t", [P, 2, P])
        wgx = sb("wgx", [P, 2, P])
        z = sb("z", [P, 2, P])
        h1 = sb("h1", [P, M1, P])
        h2 = sb("h2", [P, M2, P])
        y = sb("y", [1, BATCH])
        dense_t = sb("dense_t", [STACK_ROWS, BATCH], bf16)
        wt1 = sb("wt1", [P, 2, HID1])
        wt1d = sb("wt1d", [STACK_ROWS, HID1], bf16)
        wt2 = sb("wt2", [P, M1, HID2])
        wt3 = sb("wt3", [P, M2])
        bt1 = sb("bt1", [P, M1])
        bt2 = sb("bt2", [P, M2])
        ident = sb("ident", [P, P])
        b1c = sb("b1c", [P, 1])
        b2c = sb("b2c", [P, 1])
        b2k = sb("b2k", [P, 1])
        w2t = sb("w2t", [P, FIELDS, P])
        w1r = sb("w1r", [P, FIELDS, FIELDS])
        w1q = sb("w1q", [P, FIELDS, FIELDS])
        w1z = sb("w1z", [P, PAIRS])
        w1p = sb("w1p", [P, PAIRS])
        w1x = sb("w1x", [P, HALF * HALF])
        cb = [sb(f"cb{n}", [P, HALF, ROWS[n]]) for n in range(2)]
        cb_own = sb("cb_own", [P, HALF, OWN_ROWS])
        wpack = [[sb(f"wpack{n}{g}", [P, PACK[n]]) for g in range(2)] for n in range(2)]
        H3, G21 = HALF ** 3, G1 * G1 * G2 + G2 * G2 * G1
        fold_mem = tt[1][:, :, :].rearrange("p s b -> p (s b)")
        fold_gmem = cw[:, :, :].rearrange("p s h -> p (s h)")
        fold_half = [fold_mem[:, n * H3:(n + 1) * H3].rearrange("p (x y d) -> p x y d", x=HALF, y=HALF)
                     for n in range(2)]
        fold_group = [[None, None], [None, None]]
        for n in range(2):
            at = n * G21
            for g, (size, other) in enumerate(((G1, G2), (G2, G1))):
                fold_group[n][g] = fold_gmem[:, at:at + size * size * other].rearrange(
                    "p (x y d) -> p x y d", x=size, y=size)
                at += size * size * other
        w2r = bd[1][:, :, :, :].rearrange("p r q s -> p (r q s)")[:, 0:P * FIELDS].rearrange(
            "p (i d) -> p i d", d=FIELDS)
        dense_n = gathered[1][:, 0:TILES * DENSE].rearrange("p (t f) -> p t f", f=DENSE)
        prod_flat = [prod[h][:, :, :].rearrange("p r c -> p (r c)") for h in range(2)]
        dense_s = prod_flat[1][:, 0:TILES * STACK_ROWS].rearrange("p (t f) -> p t f", f=STACK_ROWS)
        wd = [prod_flat[0][:, i * HID1:(i + 1) * HID1] for i in range(3)]
        wd_part = [prod_flat[1][:, TILES * STACK_ROWS:].bitcast(bf16)[:, i * HID1:(i + 1) * HID1] for i in range(2)]
        dense_part = [gathered[1][:, TILES * DENSE:2 * TILES * DENSE].bitcast(bf16)[:, i * TILES * DENSE:(i + 1) *
                      TILES * DENSE].rearrange("p (t f) -> p t f", f=DENSE) for i in range(2)]

        ps_t = [[pb(f"ps_t{b}{n}", [P, 512]) for n in range(2)] for b in range(2)]
        ps_z = pb("ps_z", [P, 512])
        ps_1 = pb("ps_1", [P, 512])
        ps_2 = pb("ps_2", [P, 512])
        ps_s = pb("ps_s", [P, 512])
        z1_ps, z2_ps = ps_z[:, 0:P], ps_z[:, P:2 * P]
        y_ps = ps_2[0:1, M2 * P:(M2 + 1) * P]

        s_ids = sem("s_ids")
        s_idx0 = sem("s_idx0")
        s_w2 = sem("s_w2")
        s_w1 = sem("s_w1")
        s_dense = sem("s_dense")
        s_wd = sem("s_wd")
        s_parts = sem("s_parts")
        s_wparts = sem("s_wparts")
        s_top = sem("s_top")
        s_ident0 = sem("s_ident0")
        s_ident = sem("s_ident")
        s_const = sem("s_const")
        s_w1s = sem("s_w1s")
        s_w1p = sem("s_w1p")
        s_prep_ps = sem("s_prep_ps")
        s_prep_ev = sem("s_prep_ev")
        s_base_ps = sem("s_base_ps")
        s_base_ev = sem("s_base_ev")
        s_fold = sem("s_fold")
        s_zero = sem("s_zero")
        s_prodc = sem("s_prodc")
        s_b2 = sem("s_b2")
        idx_ready = [sem(f"idx_ready{p}") for p in range(2)]
        tile_begun = sem("tile_begun")
        gather_done = [sem(f"gather_done{p}") for p in range(2)]
        et_ready = [sem(f"et_ready{p}") for p in range(2)]
        bd_ready = [sem(f"bd_ready{p}") for p in range(2)]
        prod_ready = [sem(f"prod_ready{h}") for h in range(2)]
        half_done = [sem(f"half_done{h}") for h in range(2)]
        group_done = [sem(f"group_done{b}") for b in range(2)]
        t_copied = [sem(f"t_copied{b}") for b in range(2)]
        gx_ready = [sem(f"gx_ready{p}") for p in range(2)]
        z_done = [sem(f"z_done{p}") for p in range(2)]
        z_ready = sem("z_ready")
        top1_done = sem("top1_done")
        h1_ready = sem("h1_ready")
        top2_done = sem("top2_done")
        h2_ready = sem("h2_ready")
        y_done = sem("y_done")
        y_ready = sem("y_ready")
        s_out = sem("s_out")

        GATHERED = 16 * FIELDS
        MOVED = 16 * HALF
        prep_bank = [ps_z, ps_1, ps_2, ps_s]
        base_bank = [*prep_bank, ps_t[0][0], ps_t[0][1], ps_t[1][0], ps_t[1][1]]

        DENSE_TURNS = [range(t, t + 4) for t in range(0, TILES, 4)]
        W2_TURNS = [range(d, min(d + 4, FIELDS)) for d in range(0, FIELDS, 4)]
        pieces = [(cb[0], d, ROWS[0], S_0 + 1 + d) for d in range(HALF)]
        pieces += [(cb[1], d, ROWS[1], S_1 + d) for d in range(HALF)]
        pieces += [(cb_own, d, OWN_ROWS, S_OWN + d) for d in range(HALF)]
        CW_TURNS = [range(i, min(i + 4, len(pieces))) for i in range(0, len(pieces), 4)]
        FIRST_W2 = len(DENSE_TURNS)
        FIRST_BASE = FIRST_W2 + len(W2_TURNS)
        Z1_TURN = FIRST_BASE
        FIRST_CW = Z1_TURN + 1
        PREP = FIRST_CW + len(CW_TURNS)
        z1_pieces = [(w1z[:, BASE[n]:BASE[n] + ROWS[n]], ROWS[n], w1t[0:ROWS[n], n, :]) for n in range(2)]
        z1_pieces += [(w1x[:, GX_D[m][0] * HALF:(GX_D[m][-1] + 1) * HALF], GX_ROWS[m], wgx[0:GX_ROWS[m], m, :])
                      for m in range(2)]

        block = ctx.enter_context(nc.Block())

        @block.sync
        def _(sp):
            sp.dma_start(idx[0][:, :], ids[0:P, :]).then_inc(s_idx0, 16)
            sp.dma_start(w1r[:, :, :], w1).then_inc(s_w1, 16)
            sp.dma_start(w2r, w2).then_inc(s_w2, 16)
            sp.dma_start(ids_all[:, :, :], ids.rearrange("(t p) f -> p t f", p=P)).then_inc(s_ids, 16)

            def move_gx(k, p):
                for b in range(2):
                    sp.wait_ge(t_copied[b], 8 * k + 4 * p + 4)
                wait(sp, z_done[p], k)
                for m in range(2):
                    for j, d in enumerate(GX_D[m]):
                        sp.dma_start(gx[p][j * HALF:(j + 1) * HALF, m, :],
                                     tt[p][E_AT:E_AT + HALF, S_0 + 1 + d, :]).then_inc(gx_ready[p], 16)

            for p in range(2):
                move_gx(0, p)
            with nc.sync.Fori(1, TILES // 2) as k:
                for p in range(2):
                    move_gx(k, p)
            sp.wait_ge(y_ready, TILES)
            sp.dma_start(out.rearrange("b a -> a b"), y[:, :]).then_inc(s_out, 16)
            sp.wait_ge(s_out, 16)

        @block.gpsimd
        def _(pool):
            nc.gpsimd.memset(ident[:, :], 0.0).then_inc(s_ident0, 1)
            pool.wait_ge(s_ident0, 1)
            nc.gpsimd.affine_select(out=ident[:, :], in_=ident[:, :], compare_op=ALU.not_equal, fill=1.0, base=0,
                                    pattern=[[-1, P]], channel_multiplier=1).then_inc(s_ident, 1)

            def gather(p):
                for f in range(FIELDS):
                    pool.indirect_dma_start(
                        out=gathered[p][:, f * DIM:(f + 1) * DIM], out_offset=None, in_=tables[f],
                        in_offset=bass.IndirectOffsetOnAxis(ap=idx[p][:, f:f + 1], axis=0),
                    ).then_inc(gather_done[p], 16)

            pool.wait_ge(s_idx0, 16)
            gather(0)
            pool.wait_ge(idx_ready[1], 1)
            pool.wait_ge(s_parts, 5)
            gather(1)
            with nc.gpsimd.Fori(1, TILES // 2) as k:
                for p in range(2):
                    pool.wait_ge(idx_ready[p], k + p)
                    pool.wait_ge(et_ready[p], k)
                    nc.gpsimd.sem_inc(tile_begun, 1)
                    gather(p)

        @block.vector
        def _(dve):
            def next_indices(t, p):
                nc.vector.tensor_copy(idx[p][:, :], ids_all[:, bass.ds(t, 1), :].rearrange("p a f -> p (a f)")
                                      ).then_inc(idx_ready[p], 1)

            def diagonal_init(p):
                nc.vector.memset(bd[p][:, :, :, :], 0.0).then_inc(s_const, 1)
                dve.wait_ge(s_const, 1 + 2 * p)
                for q in range(QUADS):
                    last = nc.vector.memset(bd[p][q * DIM:(q + 1) * DIM, :, q, C_ONE:C_ONE + 1], 1.0)
                last.then_inc(s_const, 1)

            nc.vector.memset(dense_s, 0.0).then_inc(s_parts, 1)
            dve.wait_ge(s_dense, 16)
            nc.vector.tensor_copy(dense_part[0], dense_n).then_inc(s_parts, 1)
            dve.wait_ge(s_parts, 2)
            for row, part, _ in STACK:
                if part == 0:
                    nc.vector.tensor_copy(dense_s[:, :, row:row + DENSE], dense_part[0])
            nc.vector.tensor_tensor(dense_n, dense_n, dense_part[0], ALU.subtract).then_inc(s_parts, 1)
            dve.wait_ge(s_parts, 3)
            nc.vector.tensor_copy(dense_part[1], dense_n).then_inc(s_parts, 1)
            dve.wait_ge(s_parts, 4)
            for row, part, _ in STACK:
                if part == 1:
                    nc.vector.tensor_copy(dense_s[:, :, row:row + DENSE], dense_part[1])
            nc.vector.tensor_tensor(dense_s[:, :, 2 * DENSE:3 * DENSE], dense_n, dense_part[1], ALU.subtract
                                    ).then_inc(s_parts, 1)

            nc.vector.memset(w1z[:, :], 0.0).then_inc(s_w1s, 1)
            dve.wait_ge(s_w1, 32)
            nc.vector.tensor_tensor(w1q[:, :, :], w1r[:, :, :], w1r[:, :, :].rearrange("p x y -> p y x"),
                                    ALU.add).then_inc(s_w1s, 1)
            dve.wait_ge(s_w1s, 2)
            diag = slice(0, FIELDS * FIELDS, FIELDS + 1)
            nc.vector.tensor_copy(w1q[:, :, :].rearrange("p x y -> p (x y)")[:, diag],
                                  w1r[:, :, :].rearrange("p x y -> p (x y)")[:, diag]).then_inc(s_w1s, 1)
            dve.wait_ge(s_w1s, 3)
            for n in range(2):
                f0 = n * HALF
                for q in range(HALF):
                    row, p0 = within_row(q)
                    at = BASE[n] + W_AT[n] + row
                    nc.vector.tensor_copy(w1z[:, at:at + q - p0 + 1], w1q[:, f0 + q, f0 + p0:f0 + q + 1])
                at = BASE[n] + X_AT[n]
                nc.vector.tensor_copy(w1z[:, at:at + ACROSS].rearrange("p (y x) -> p y x", x=G1),
                                      w1q[:, f0 + G1:f0 + HALF, f0:f0 + G1])
            nc.vector.tensor_copy(w1x[:, :].rearrange("p (d a) -> p d a", a=HALF), w1q[:, HALF:, 0:HALF])
            nc.vector.tensor_copy(w1z[:, ONE_AT[0]:ONE_AT[0] + 1], b1c[:, :]).then_inc(s_w1s, 1)
            dve.wait_ge(s_w1s, 4)
            nc.vector.tensor_copy(w1p[:, :], w1z[:, :]).then_inc(s_w1s, 1)
            dve.wait_ge(s_w1s, 5)
            at = BASE[1] + ONE_AT[1]
            nc.vector.tensor_copy(w1p[:, at:at + 1], b1c[:, :]).then_inc(s_w1s, 1)
            dve.wait_ge(s_w1s, 6)
            for n in range(2):
                own, other = (slice(m * HALF, (m + 1) * HALF) for m in (n, 1 - n))
                for g in range(2):
                    w = wpack[n][g]
                    y0, y1 = (n * HALF + v for v in GROUP_OF[g])
                    d0, d1 = (n * HALF + v for v in GROUP_OF[1 - g])
                    at = BASE[n] + W_AT[n]
                    nc.vector.tensor_copy(w[:, AT_OWN[n]:AT_FH[n]], w1z[:, at:at + WITHIN])
                    nc.vector.tensor_copy(w[:, AT_FH[n]:AT_FG[n]].rearrange("p (y d) -> p y d", d=HALF),
                                          w1q[:, own, other])
                    nc.vector.tensor_copy(w[:, AT_FG[n]:PACK[n]].rearrange("p (y d) -> p y d", d=d1 - d0),
                                          w1q[:, y0:y1, d0:d1])
                    last = nc.vector.tensor_copy(w[:, 0:ROWS[1 - n]], w1p[:, BASE[1 - n]:BASE[1 - n] + ROWS[1 - n]])
            last.then_inc(s_w1p, 1)
            dve.wait_ge(s_ids, 16)
            next_indices(1, 1)
            diagonal_init(0)
            nc.vector.memset(cb_own[:, :, WITHIN:P // 2], 0.0)
            nc.vector.memset(tt[0][P // 4:P // 2, S_OWN:, :], 0.0).then_inc(s_zero, 1)
            dve.wait_ge(s_prep_ps, FIRST_BASE)
            diagonal_init(1)

            lower = slice(64, STACK_ROWS)
            nc.vector.memset(wt1d[32:64, :], 0.0).then_inc(s_wparts, 1)
            dve.wait_ge(s_wd, 16 * len(STACK))
            nc.vector.tensor_copy(wd_part[0][lower], wd[0][lower]).then_inc(s_wparts, 1)
            dve.wait_ge(s_wparts, 2)
            nc.vector.tensor_copy(wt1d[0:3 * DENSE, :], wd[0][0:3 * DENSE])
            nc.vector.tensor_tensor(wd[1][lower], wd[0][lower], wd_part[0][lower], ALU.subtract).then_inc(s_wparts, 1)
            dve.wait_ge(s_wparts, 3)
            nc.vector.tensor_copy(wd_part[1][lower], wd[1][lower]).then_inc(s_wparts, 1)
            dve.wait_ge(s_wparts, 4)
            nc.vector.tensor_copy(wt1d[64:96, :], wd_part[1][64:96])
            nc.vector.tensor_tensor(wd[2][lower], wd[1][lower], wd_part[1][lower], ALU.subtract).then_inc(s_wparts, 1)
            dve.wait_ge(s_wparts, 5)
            nc.vector.tensor_copy(wt1d[96:STACK_ROWS, :], wd[2][96:STACK_ROWS]).then_inc(s_wparts, 1)

            dve.wait_ge(s_wparts, 6)
            for h in range(2):
                for n in range(2):
                    at = BASE[n] + ONE_AT[n]
                    nc.vector.memset(prod[h][:, :, at:at + 1], 1.0)
                last = nc.vector.memset(prod[h][:, :, BASE[1] + ACROSS + 1:BASE[1] + W_AT[1]], 0.0)
            last.then_inc(s_prodc, 1)

            def fold(second):
                for n in range(2):
                    for q in range(HALF):
                        row, p0 = within_row(q)
                        g = int(q >= G1)
                        count = q - p0 + 1 - second
                        if not count:
                            continue
                        o = cb[n][:, :, W_AT[n] + row:W_AT[n] + row + count]
                        o_own = cb_own[:, GROUP_OF[1 - g][0]:GROUP_OF[1 - g][1], W_AT[n] + row:W_AT[n] + row + count]
                        fh, fg = fold_half[n], fold_group[n][g]
                        if second:
                            term = fh[:, q, p0:q, :].rearrange("p y d -> p d y")
                            term_own = fg[:, q - p0, 0:q - p0, :].rearrange("p y d -> p d y")
                        else:
                            term = fh[:, p0:q + 1, q, :].rearrange("p x d -> p d x")
                            term_own = fg[:, 0:q - p0 + 1, q - p0, :].rearrange("p x d -> p d x")
                        nc.vector.tensor_tensor(o, o, term, ALU.add)
                        nc.vector.tensor_tensor(o_own, o_own, term_own, ALU.add)
                    o = cb[n][:, :, X_AT[n]:X_AT[n] + ACROSS].rearrange("p d (y x) -> p d y x", x=G1)
                    if second:
                        term = fold_half[n][:, G1:, 0:G1, :].rearrange("p x y d -> p d x y")
                    else:
                        term = fold_half[n][:, 0:G1, G1:, :].rearrange("p x y d -> p d y x")
                    last = nc.vector.tensor_tensor(o, o, term, ALU.add)
                last.then_inc(s_fold, 1)

            def tile(k, p):
                t = 2 * k + p
                dve.wait_ge(gather_done[p], GATHERED * (k + 1))
                wait(dve, bd_ready[p], 2 * k)
                wait(dve, prod_ready[1], t)
                nc.vector.transpose(et[p][:, :, :].rearrange("p r f -> p f r"),
                                    gathered[p][:, :].rearrange("p (f k) -> p f k", k=DIM)).then_inc(et_ready[p], 1)
                if not isinstance(k, int) or k < TILES // 2 - 1:
                    next_indices(t + 2, p)
                dve.wait_ge(et_ready[p], k + 1)
                for h in range(2):
                    wait(dve, half_done[h], t)
                    e = et[p][:, h * HR:(h + 1) * HR, :]
                    for n in range(2):
                        f0 = n * HALF
                        for q in range(HALF):
                            row, p0 = within_row(q)
                            at, count = BASE[n] + W_AT[n] + row, q - p0 + 1
                            nc.vector.tensor_tensor(
                                prod[h][:, :, at:at + count], e[:, :, f0 + p0:f0 + q + 1],
                                e[:, :, f0 + q:f0 + q + 1].broadcast_to([P, HR, count]), ALU.mult)
                        at = BASE[n] + X_AT[n]
                        nc.vector.tensor_tensor(
                            prod[h][:, :, at:at + ACROSS].rearrange("p r (y x) -> p r y x", x=G1),
                            e[:, :, f0:f0 + G1].unsqueeze(2).broadcast_to([P, HR, G2, G1]),
                            e[:, :, f0 + G1:f0 + HALF].unsqueeze(3).broadcast_to([P, HR, G2, G1]), ALU.mult)
                    nc.vector.tensor_copy(prod[h][:, :, E_AT:E_AT + HALF], e[:, :, 0:HALF]).then_inc(prod_ready[h], 1)

            tile(0, 0)
            dve.wait_ge(s_base_ev, FIELDS)
            fold(0)
            dve.wait_ge(s_fold, 1)
            fold(1)
            dve.wait_ge(s_fold, 2)
            nc.vector.memset(tt[1][P // 4:P // 2, S_OWN:, :], 0.0).then_inc(s_zero, 1)
            tile(0, 1)
            with nc.vector.Fori(1, TILES // 2 - 1) as k:
                for p in range(2):
                    tile(k, p)
            for p in range(2):
                tile(TILES // 2 - 1, p)

        @block.scalar
        def _(act):
            act.dma_start(b1c[:, :], b1.rearrange("(p a) -> p a", a=1)).then_inc(s_w1, 16)
            act.dma_start(dense_n, dense.rearrange("(t p) f -> p t f", p=P)).then_inc(s_dense, 16)
            act.dma_start(wt1[:, :, :], w_top1[0:2 * P, :].rearrange("(c p) n -> p c n", p=P)).then_inc(s_top, 16)
            for row, _, _ in STACK:
                act.dma_start(wd[0][row:row + DENSE, :], w_top1[2 * P:, :]).then_inc(s_wd, 16)
            act.dma_start(wt2[:, :, :], w_top2.rearrange("(c p) n -> p c n", p=P)).then_inc(s_top, 16)
            with nc.allow_non_contiguous_dma(reason="a few hundred biases, once"):
                act.dma_start(wt3[:, :], w_top3.rearrange("(c p) a -> p (c a)", p=P)).then_inc(s_top, 16)
                act.dma_start(bt1[:, :], b_top1.rearrange("(c p) -> p c", p=P)).then_inc(s_top, 16)
                act.dma_start(bt2[:, :], b_top2.rearrange("(c p) -> p c", p=P)).then_inc(s_top, 16)
            act.dma_start(b2c[:, :], b2.rearrange("(p a) -> p a", a=1)).then_inc(s_top, 16)

            def copy(dst, src):
                return nc.scalar.activation(dst, src, ACT.Copy)

            for i, ts in enumerate(DENSE_TURNS):
                act.wait_ge(s_prep_ps, i + 1)
                copy(dense_t[:, ts[0] * P:(ts[-1] + 1) * P],
                     prep_bank[i % 4][0:STACK_ROWS, 0:len(ts) * P]).then_inc(s_prep_ev, 1)
            for i, ds in enumerate(W2_TURNS):
                turn = FIRST_W2 + i
                act.wait_ge(s_prep_ps, turn + 1)
                copy(w2t[:, ds[0]:ds[-1] + 1, :].rearrange("p d h -> p (d h)"),
                     prep_bank[turn % 4][:, 0:len(ds) * P]).then_inc(s_prep_ev, 1)
            for x in range(FIELDS):
                n, q = x // HALF, x % HALF
                g = int(q >= G1)
                bank, size, other = base_bank[x % 8], *((G1, G2) if g == 0 else (G2, G1))
                act.wait_ge(s_base_ps, x + 1)
                copy(cb[1 - n][:, q, :], bank[:, 0:ROWS[1 - n]])
                copy(cb_own[:, q, W_AT[n]:W_AT[n] + WITHIN], bank[:, AT_OWN[n]:AT_FH[n]])
                copy(fold_half[n][:, q, :, :].rearrange("p y d -> p (y d)"), bank[:, AT_FH[n]:AT_FG[n]])
                copy(fold_group[n][g][:, q - GROUP_OF[g][0], :, :].rearrange("p y d -> p (y d)"),
                     bank[:, AT_FG[n]:PACK[n]]).then_inc(s_base_ev, 1)
            act.wait_ge(s_prep_ps, Z1_TURN + 1)
            for j, (_, rows, dst) in enumerate(z1_pieces):
                last = copy(dst, prep_bank[Z1_TURN % 4][0:rows, j * P:(j + 1) * P])
            last.then_inc(s_prep_ev, 1)
            act.wait_ge(s_top, 16 * 6)
            nc.scalar.mul(b2k[:, :], b2c[:, :], float(DIM)).then_inc(s_b2, 1)

            def fields_out(k, p):
                act.wait_ge(et_ready[p], k + 1)
                wait(act, half_done[1], 2 * k + p)
                for h in range(2):
                    rs = slice(h * HR, (h + 1) * HR)
                    for q in range(QUADS):
                        rows = slice(q * DIM, (q + 1) * DIM)
                        for f0, c0 in ((0, 0), (HALF, C_B)):
                            last = copy(bd[p][rows, rs, q, c0:c0 + HALF], et[p][rows, rs, f0:f0 + HALF])
                    last.then_inc(bd_ready[p], 1)

            def triples_out(k, p):
                wait(act, z_done[p], k)
                wait(act, gx_ready[p], MOVED * k)
                for g in range(GROUPS):
                    b = g % 2
                    if g % GPH == GPH - 1:
                        act.wait_ge(half_done[g // GPH], 2 * k + p + 1)
                    elif b:
                        act.wait_ge(group_done[1], 4 * k + 2 * p + g // GPH + 1)
                    else:
                        act.wait_ge(group_done[0], 8 * k + 4 * p + g // 2 + 1)
                    samples = slice(g * GR, (g + 1) * GR)
                    own = [(n, slice(W_AT[n], W_AT[n] + WITHIN), S_OWN, n * C_B, HALF) for n in range(2)]
                    for n, rows, s0, c0, count in (
                            (0, slice(0, ROWS[0]), S_0, C_ONE, HALF + 1), (1, slice(0, ROWS[1]), S_1, 0, HALF + 1), *own):
                        last = copy(
                            tt[p][rows, s0:s0 + count, :].rearrange("p s (q r) -> p s q r", q=QUADS)[:, :, :, samples],
                            ps_t[b][n][rows, 0:GR * QUADS * COLS].rearrange(
                                "p (r q s) -> p s q r", q=QUADS, s=COLS)[:, c0:c0 + count, :, :])
                    last.then_inc(t_copied[b], 1)

            def z_out(k, p):
                act.wait_ge(z_done[p], k + 1)
                wait(act, top1_done, 2 * k + p)
                copy(z[:, 0, :], z1_ps)
                nc.scalar.activation(z[:, 1, :], z2_ps, ACT.Identity, bias=b2k[:, 0:1]).then_inc(z_ready, 1)

            def mlp_out(t):
                act.wait_ge(top1_done, t + 1)
                wait(act, top2_done, t)
                for m in range(M1):
                    last = nc.scalar.activation(h1[:, m, :], ps_1[:, m * P:(m + 1) * P], ACT.Relu,
                                                bias=bt1[:, m:m + 1])
                last.then_inc(h1_ready, 1)
                act.wait_ge(top2_done, t + 1)
                wait(act, y_done, t)
                for m in range(M2):
                    last = nc.scalar.activation(h2[:, m, :], ps_2[:, m * P:(m + 1) * P], ACT.Relu,
                                                bias=bt2[:, m:m + 1])
                last.then_inc(h2_ready, 1)
                act.wait_ge(y_done, t + 1)
                copy(y[:, bass.ds(t * P, P)], y_ps).then_inc(y_ready, 1)

            act.wait_ge(s_const, 4)
            fields_out(0, 0)
            act.wait_ge(s_zero, 1)
            act.wait_ge(s_b2, 1)
            triples_out(0, 0)
            for i, turn_pieces in enumerate(CW_TURNS):
                act.wait_ge(s_prep_ps, FIRST_CW + i + 1)
                bank = prep_bank[(FIRST_CW + i) % 4]
                runs = []
                for j, c in enumerate(turn_pieces):
                    if runs and pieces[runs[-1][0]][2] == pieces[c][2]:
                        runs[-1][2] += 1
                    else:
                        runs.append([c, j, 1])
                for c, j, count in runs:
                    rows = pieces[c][2]
                    last = copy(cw[0:rows, c:c + count, :].rearrange("p s h -> p (s h)"),
                                bank[0:rows, j * P:(j + count) * P])
                last.then_inc(s_prep_ev, 1)
            fields_out(0, 1)
            z_out(0, 0)

            def tile(k, p, t):
                triples_out(k, p)
                mlp_out(t - 1)
                fields_out(k + p, 1 - p)
                z_out(k, p)

            act.wait_ge(s_zero, 2)
            tile(0, 1, 1)
            tile(1, 0, 2)
            with nc.scalar.Fori(1, TILES // 2 - 1) as k:
                tile(k, 1, 2 * k + 1)
                tile(k + 1, 0, 2 * k + 2)
            triples_out(TILES // 2 - 1, 1)
            mlp_out(TILES - 2)
            z_out(TILES // 2 - 1, 1)
            mlp_out(TILES - 1)

        @block.tensor
        def _(pe):
            def turn_free(turn):
                wait(pe, s_prep_ev, turn - 3)

            pe.wait_ge(s_ident, 1)
            pe.wait_ge(s_parts, 5)
            for i, ts in enumerate(DENSE_TURNS):
                turn_free(i)
                for j, t in enumerate(ts):
                    last = nc.tensor.transpose(prep_bank[i % 4][0:STACK_ROWS, j * P:(j + 1) * P], dense_s[:, t, :],
                                               ident[:, :])
                last.then_inc(s_prep_ps, 1)
            pe.wait_ge(s_w2, 16)
            for i, ds in enumerate(W2_TURNS):
                turn = FIRST_W2 + i
                turn_free(turn)
                for j, d in enumerate(ds):
                    last = nc.tensor.transpose(prep_bank[turn % 4][:, j * P:(j + 1) * P], w2r[:, :, d], ident[:, :])
                last.then_inc(s_prep_ps, 1)
            pe.wait_ge(s_w1p, 1)
            pe.wait_ge(s_prep_ev, FIRST_BASE)
            for x in range(FIELDS):
                n, g = x // HALF, int(x % HALF >= G1)
                wait(pe, s_base_ev, x - 7)
                nc.tensor.matmul(base_bank[x % 8][:, 0:PACK[n]], w2t[:, x, :], wpack[n][g][:, :],
                                 start=True, stop=True).then_inc(s_base_ps, 1)
            pe.wait_ge(s_base_ev, FIELDS)
            turn_free(Z1_TURN)
            for j, (src, rows, _) in enumerate(z1_pieces):
                last = nc.tensor.transpose(prep_bank[Z1_TURN % 4][0:rows, j * P:(j + 1) * P], src, ident[:, :])
            last.then_inc(s_prep_ps, 1)

            def triples(k, p):
                for g in range(GROUPS):
                    h, b = g // GPH, g % 2
                    if g % GPH == 0:
                        pe.wait_ge(bd_ready[p], 2 * k + h + 1)
                        pe.wait_ge(prod_ready[h], 2 * k + p + 1)
                    wait(pe, t_copied[b], 8 * k + 4 * p + g // 2)
                    for j in range(GR):
                        r = g * GR + j
                        for n in range(2):
                            last = nc.tensor.matmul(
                                ps_t[b][n][0:ROWS[n], j * QUADS * COLS:(j + 1) * QUADS * COLS],
                                prod[h][:, r - h * HR, BASE[n]:BASE[n] + ROWS[n]],
                                bd[p][:, r, :, :].rearrange("p q s -> p (q s)"), start=True, stop=True)
                    if g % GPH == GPH - 1:
                        last.then_inc(half_done[h], 1)
                    else:
                        last.then_inc(group_done[b], 1)

            N_PIECES = len(pieces)

            def z2_part(p, lo, hi):
                for i in range(lo, hi):
                    _, _, rows, s = pieces[i]
                    nc.tensor.matmul(z2_ps, cw[0:rows, i, :], tt[p][0:rows, s, :],
                                     start=(i == 0), stop=(i == N_PIECES - 1))

            def z_begin(k, p):
                for b in range(2):
                    pe.wait_ge(t_copied[b], 8 * k + 4 * p + 4)
                wait(pe, z_ready, 2 * k + p)

            def z1_part(k, p):
                for n in range(2):
                    nc.tensor.matmul(z1_ps, w1t[0:ROWS[n], n, :], tt[p][0:ROWS[n], SLOT_ONE[n], :],
                                     start=(n == 0), stop=False)
                pe.wait_ge(gx_ready[p], MOVED * (k + 1))
                for m in range(2):
                    last = nc.tensor.matmul(z1_ps, wgx[0:GX_ROWS[m], m, :], gx[p][0:GX_ROWS[m], m, :],
                                            start=False, stop=(m == 1))
                last.then_inc(z_done[p], 1)

            def top1(t):
                pe.wait_ge(z_ready, t + 1)
                wait(pe, h1_ready, t)
                for m in range(M1):
                    cols = slice(m * P, (m + 1) * P)
                    nc.tensor.matmul(ps_1[:, cols], wt1d[:, cols], dense_t[:, bass.ds(t * P, P)],
                                     start=True, stop=False)
                    nc.tensor.matmul(ps_1[:, cols], wt1[:, 0, cols], z[:, 0, :], start=False, stop=False)
                    last = nc.tensor.matmul(ps_1[:, cols], wt1[:, 1, cols], z[:, 1, :], start=False, stop=True)
                last.then_inc(top1_done, 1)

            def top2(t):
                pe.wait_ge(h1_ready, t + 1)
                wait(pe, h2_ready, t)
                wait(pe, y_ready, t)
                for m in range(M2):
                    for c in range(M1):
                        last = nc.tensor.matmul(ps_2[:, m * P:(m + 1) * P], wt2[:, c, m * P:(m + 1) * P], h1[:, c, :],
                                                start=(c == 0), stop=(c == M1 - 1))
                last.then_inc(top2_done, 1)

            def top3(t):
                pe.wait_ge(h2_ready, t + 1)
                for c in range(M2):
                    last = nc.tensor.matmul(y_ps, wt3[:, c:c + 1], h2[:, c, :], start=(c == 0), stop=(c == M2 - 1))
                last.then_inc(y_done, 1)

            def tile(k, p, t):
                triples(k, p)
                top1(t - 1)
                z_begin(k, p)
                z2_part(p, 0, N_PIECES // 2)
                top2(t - 1)
                z2_part(p, N_PIECES // 2, N_PIECES * 3 // 4)
                top3(t - 1)
                z2_part(p, N_PIECES * 3 // 4, N_PIECES)
                z1_part(k, p)

            pe.wait_ge(s_prodc, 1)
            triples(0, 0)
            pe.wait_ge(s_fold, 2)
            for i, turn_pieces in enumerate(CW_TURNS):
                turn = FIRST_CW + i
                turn_free(turn)
                for j, c in enumerate(turn_pieces):
                    src, d, rows, _ = pieces[c]
                    last = nc.tensor.transpose(prep_bank[turn % 4][0:rows, j * P:(j + 1) * P], src[:, d, :],
                                               ident[:, :])
                last.then_inc(s_prep_ps, 1)
            pe.wait_ge(s_prep_ev, PREP)
            z_begin(0, 0)
            z2_part(0, 0, N_PIECES)
            z1_part(0, 0)
            pe.wait_ge(s_top, 16 * 6)
            pe.wait_ge(s_wparts, 6)
            tile(0, 1, 1)
            tile(1, 0, 2)
            with nc.tensor.Fori(1, TILES // 2 - 1) as k:
                tile(k, 1, 2 * k + 1)
                tile(k + 1, 0, 2 * k + 2)
            tile(TILES // 2 - 1, 1, TILES - 1)
            top1(TILES - 1)
            top2(TILES - 1)
            top3(TILES - 1)


TABLES = [f"tbl_{f}" for f in range(FIELDS)]
INPUTS = ["dense_ctx", "ids", *TABLES, "W_top1", "b_top1", "W_top2", "b_top2", "W_top3",
          "L0_rec_W1", "L0_rec_b1", "L0_rec_W2", "L0_rec_b2"]


def kernel(**inputs):
    import numpy as np
    import concourse.bacc as bacc
    from concourse import mybir
    from concourse.bass_utils import run_bass_kernel_spmd

    nc = bacc.Bacc("TRN2", target_bir_lowering=False, num_devices=1)
    arrays, ap = {}, {}
    for name in INPUTS:
        a = np.ascontiguousarray(inputs[name])
        arrays[f"in_{name}"] = a
        ap[name] = nc.dram_tensor(f"in_{name}", a.shape, mybir.dt.from_np(a.dtype), kind="ExternalInput").ap()
    out = nc.dram_tensor("out", (BATCH, 1), mybir.dt.float32, kind="ExternalOutput").ap()
    build(nc, ap["dense_ctx"], ap["ids"], [ap[t] for t in TABLES], ap["W_top1"], ap["b_top1"], ap["W_top2"],
          ap["b_top2"], ap["W_top3"], ap["L0_rec_W1"], ap["L0_rec_b1"], ap["L0_rec_W2"], ap["L0_rec_b2"], out)
    result = run_bass_kernel_spmd(nc, [arrays], core_ids=[0])
    return result.results[0]["out"]
```

```python
from contextlib import ExitStack

import concourse.bass as bass
from concourse import mybir

P = 128
BATCH, FIELDS, DIM = 2048, 26, 32
TILES = BATCH // P
QUADS = P // DIM
DENSE, HID1, HID2 = 16, 512, 256
M1, M2 = HID1 // P, HID2 // P

STACK = [(0, 0, 0), (DENSE, 1, 0), (2 * DENSE, 2, 0), (64, 0, 1), (64 + DENSE, 1, 1), (96, 0, 2)]
STACK_ROWS = 96 + DENSE

HALF = FIELDS // 2
K0, L0, U0, V0 = 0, 4, 8, 9
GROUP_OF = [(K0, L0), (L0, U0), (U0, V0), (V0, HALF)]
BLOCK = 32
WITHIN = sum((b - a) * (b - a + 1) // 2 for a, b in GROUP_OF)
KL, KLU = (L0 - K0) * (U0 - L0), U0 - K0
KEPT = KL + KLU
ACROSS = HALF * (HALF + 1) // 2 - WITHIN

ONE_AT, X_AT = WITHIN, BLOCK
E_AT = BLOCK + ACROSS
ROWS = [E_AT + HALF, E_AT]
BASE = [0, ROWS[0]]
PAIRS = ROWS[0] + ROWS[1]

COLS = FIELDS + 1
C_ONE, C_B = HALF, HALF + 1
OWN_BLOCKS = HALF + HALF - U0
OWN_SLOTS = OWN_BLOCKS // 2
S_0, S_1, S_OWN = 0, HALF + 1, 2 * (HALF + 1)
NSLOT = S_OWN + OWN_SLOTS
SLOT_ONE = [S_0, S_1 + HALF]

TERMS_W = [(b - a) * (HALF - (b - a)) for a, b in GROUP_OF]
TERMS_X = [(U0 - L0) * (HALF - U0) + HALF - V0, (L0 - K0) * (HALF - U0) + HALF - V0, KLU * (HALF - V0), 0]
TERMS = [w + x for w, x in zip(TERMS_W, TERMS_X)]
SPEC = [TERMS[0], TERMS[1], TERMS[2] + KEPT, TERMS[3] + KEPT]
AT_OWN = [ROWS[1], ROWS[0]]
AT_FH = [c + WITHIN for c in AT_OWN]
COMMON = [c + HALF * HALF for c in AT_FH]
WPACK = [[SPEC[g] + COMMON[n] + SPEC[g + 1] for g in (0, 2)] for n in range(2)]


def group(q):
    return [g for g, (a, b) in enumerate(GROUP_OF) if a <= q < b][0]


def bank_columns(n, g):
    return (SPEC[g], 0) if g % 2 == 0 else (0, COMMON[n])


HOT = [2, 10]
HOT_ROWS = 8
HOTS = len(HOT)
HOT_FIELDS = slice(HOT[0], HOT[-1] + 1, HOT[1] - HOT[0])
PARTS = 3
FIRST_HOT = 2

HR = DIM // 2
GR = 4
GROUPS = DIM // GR
GPH = GROUPS // 2

GX = [P, 2 + 2 * HALF, HALF]
GX_AT = [0, ROWS[1], ROWS[0]]
GX_FIRST = [0, GX[0], GX[0] + GX[1]]
Z1_ROWS = [ROWS[0] + GX[2], ROWS[1] + GX[1]]


def within_row(q):
    row = 0
    for a, b in GROUP_OF:
        if q < b:
            return row + (q - a) * (q - a + 1) // 2, a
        row += (b - a) * (b - a + 1) // 2


CROSS = [(0, (L0, U0), (K0, L0)), (KL, (U0, V0), (K0, U0)), (KEPT, (V0, HALF), (K0, V0))]


def others(g):
    a, b = GROUP_OF[g]
    cut = [(0, a, 0), (b, OWN_SLOTS, a), (max(b, OWN_SLOTS), HALF, max(b, OWN_SLOTS) - (b - a))]
    if a >= OWN_SLOTS:
        cut = [(0, a, 0)]
    return [r for r in cut if r[0] < r[1]]


def own_block(n, i):
    return i % OWN_SLOTS, 2 * n + i // OWN_SLOTS


def wait(engine, sem, count):
    if not isinstance(count, int) or count > 0:
        engine.wait_ge(sem, count)


def build(nc, dense, ids, tables, w_top1, b_top1, w_top2, b_top2, w_top3, w1, b1, w2, b2, out):
    f32, bf16, f16, i32 = mybir.dt.float32, mybir.dt.bfloat16, mybir.dt.float16, mybir.dt.int32
    HOT_P = tables[HOT[0]].shape[0] // HOT_ROWS
    for f in HOT:
        assert HOT_P * HOT_ROWS == tables[f].shape[0] <= 2048
    ALU, ACT = mybir.AluOpType, mybir.ActivationFunctionType
    ctx = ExitStack()
    with ctx:
        def sb(name, shape, dt=f32):
            return ctx.enter_context(nc.sbuf_tensor(name, shape, dt))

        def pb(name, shape):
            return ctx.enter_context(nc.psum_tensor(name, shape, f32))

        def sem(name):
            return ctx.enter_context(nc.semaphore(name))

        ids_all = sb("ids_all", [P, TILES, FIELDS], i32)
        idx = [sb(f"idx{p}", [P, FIELDS], i32) for p in range(2)]
        gathered = [sb(f"gathered{p}", [P, FIELDS * DIM]) for p in range(2)]
        et = [sb(f"et{p}", [P, DIM, FIELDS]) for p in range(2)]
        bd = [sb(f"bd{p}", [P, DIM, QUADS, COLS]) for p in range(2)]
        prod = [sb(f"prod{h}", [P, HR, PAIRS]) for h in range(2)]
        tt = [sb(f"tt{p}", [P, NSLOT, P]) for p in range(2)]
        gx = [sb(f"gx{p}", [P, P]) for p in range(2)]
        cw = sb("cw", [P, 2 * HALF + OWN_SLOTS, P])
        w1t = sb("w1t", [P, 2, P])
        wgx = sb("wgx", [P, P])
        z = sb("z", [P, 2, P])
        h1 = sb("h1", [P, M1, P])
        h2 = sb("h2", [P, M2, P])
        y = sb("y", [1, BATCH])
        dense_t = sb("dense_t", [STACK_ROWS, BATCH], bf16)
        wt1 = sb("wt1", [P, 2, HID1])
        wt1d = sb("wt1d", [STACK_ROWS, HID1], bf16)
        wt2 = sb("wt2", [P, M1, HID2])
        wt3 = sb("wt3", [P, M2])
        bt1 = sb("bt1", [P, M1])
        bt2 = sb("bt2", [P, M2])
        ident = sb("ident", [P, P])
        ident16 = sb("ident16", [P, P], f16)
        hot_table = sb("hot_table", [HOT_P, HOTS, HOT_ROWS, PARTS, DIM], bf16)
        row_i = sb("row_i", [HOT_P, HOT_ROWS], i32)
        row_no = sb("row_no", [HOT_P, HOT_ROWS])
        hot_ids = sb("hot_ids", [P, HOTS, HOT_P], f16)
        one_hot = sb("one_hot", [HOT_P, HOTS, HOT_ROWS, P], bf16)
        b1c = sb("b1c", [P, 1])
        b2c = sb("b2c", [P, 1])
        b2k = sb("b2k", [P, 1])
        w2t = sb("w2t", [P, FIELDS, P])
        w1r = sb("w1r", [P, FIELDS, FIELDS])
        w1q = sb("w1q", [P, FIELDS, FIELDS])
        w1z = sb("w1z", [P, PAIRS])
        w1p = sb("w1p", [P, PAIRS])
        w1x = sb("w1x", [P, HALF * HALF])
        w1o = [sb(f"w1o{n}", [P, Z1_ROWS[n]]) for n in range(2)]
        cb_all = sb("cb", [P, 2, HALF, ROWS[0]])
        cb = [cb_all[:, n, :, 0:ROWS[n]] for n in range(2)]
        cb_own = sb("cb_own", [P, OWN_SLOTS, QUADS, BLOCK])
        wpack = [[sb(f"wpack{n}{i}", [P, WPACK[n][i]]) for i in range(2)] for n in range(2)]
        H3, STRIPE, STRIPE_UV = HALF ** 3, max(TERMS), max(TERMS[2:])
        fold_mem = tt[1][:, :, :].rearrange("p s b -> p (s b)")
        fold_half = fold_mem[:, 0:2 * H3].rearrange("p (n x y d) -> p n x y d", n=2, x=HALF, y=HALF)
        fold_kl = cw[:, 2 * HALF:, :].rearrange("p s h -> p (s h)")[:, 0:2 * U0 * STRIPE].rearrange(
            "p (n x c) -> p n x c", n=2, x=U0)
        fold_uv = w1r[:, :, :].rearrange("p x y -> p (x y)")[:, 0:2 * (HALF - U0) * STRIPE_UV].rearrange(
            "p (n x c) -> p n x c", n=2, x=HALF - U0)

        def fold_own(x0, x1, c0, c1):
            if x0 < U0:
                return fold_kl[:, :, x0:x1, c0:c1]
            return fold_uv[:, :, x0 - U0:x1 - U0, c0:c1]

        w2r = bd[1][:, :, :, :].rearrange("p r q s -> p (r q s)")[:, 0:P * FIELDS].rearrange(
            "p (i d) -> p i d", d=FIELDS)
        dense_n = gathered[1][:, 0:TILES * DENSE].rearrange("p (t f) -> p t f", f=DENSE)
        hot_n = [b[0:HOT_P, :, :].rearrange("p m s -> p (m s)")[:, 0:HOT_ROWS * DIM].rearrange(
            "p (c d) -> p c d", d=DIM) for b in (h2, z)]
        wd = h1[:, :, :].rearrange("p m s -> p (m s)")
        dense_s = prod[1][:, :, :].rearrange("p r c -> p (r c)")[:, 0:TILES * STACK_ROWS].rearrange(
            "p (t f) -> p t f", f=STACK_ROWS)
        dense_part = [gathered[1][:, TILES * DENSE:2 * TILES * DENSE].bitcast(bf16)[:, i * TILES * DENSE:(i + 1) *
                      TILES * DENSE].rearrange("p (t f) -> p t f", f=DENSE) for i in range(2)]

        ps_t = [[pb(f"ps_t{b}{n}", [P, 512]) for n in range(2)] for b in range(2)]
        ps_z = pb("ps_z", [P, 512])
        ps_1 = pb("ps_1", [P, 512])
        ps_2 = pb("ps_2", [P, 512])
        ps_s = pb("ps_s", [P, 512])
        spread_ps = ps_s[0:HOT_P, 0:HOTS * P]
        picked_ps = ps_s[:, HOTS * P:HOTS * (P + PARTS * DIM)]
        z1_ps, z2_ps = ps_z[:, 0:P], ps_z[:, P:2 * P]
        y_ps = ps_2[0:1, M2 * P:(M2 + 1) * P]
        last1_ps = [ps_t[m // 2][m % 2][:, 0:P] for m in range(M1)]
        last2_ps = [ps_1[:, 0:P], ps_2[:, 0:P]]
        last_y_ps = ps_s[0:1, 0:P]

        s_ids = sem("s_ids")
        s_idx0 = sem("s_idx0")
        s_w2 = sem("s_w2")
        s_w1 = sem("s_w1")
        s_dense = sem("s_dense")
        s_wd = sem("s_wd")
        s_parts = sem("s_parts")
        s_wparts = sem("s_wparts")
        s_top = sem("s_top")
        s_ident0 = sem("s_ident0")
        s_ident = sem("s_ident")
        s_const = sem("s_const")
        s_w1s = sem("s_w1s")
        s_w1p = sem("s_w1p")
        s_prep_ps = sem("s_prep_ps")
        s_prep_ev = sem("s_prep_ev")
        s_base_ps = sem("s_base_ps")
        s_base_ev = sem("s_base_ev")
        s_fold = sem("s_fold")
        s_prodc = sem("s_prodc")
        s_b2 = sem("s_b2")
        idx_ready = [sem(f"idx_ready{p}") for p in range(2)]
        tile_begun = sem("tile_begun")
        gather_done = [[sem(f"gather_done{p}{n}") for n in range(2)] for p in range(2)]
        et_ready = [sem(f"et_ready{p}") for p in range(2)]
        s_hot = sem("s_hot")
        s_hot_parts = sem("s_hot_parts")
        s_rows = sem("s_rows")
        hot_ids_ready = sem("hot_ids_ready")
        ids_spread = sem("ids_spread")
        one_hot_ready = sem("one_hot_ready")
        rows_picked = sem("rows_picked")
        rows_placed = sem("rows_placed")
        bd_ready = [sem(f"bd_ready{p}") for p in range(2)]
        prod_ready = [sem(f"prod_ready{h}") for h in range(2)]
        t_done = [sem(f"t_done{n}") for n in range(2)]
        t_copied = [sem(f"t_copied{n}") for n in range(2)]
        gx_ready = [sem(f"gx_ready{p}") for p in range(2)]
        z_done = [sem(f"z_done{p}") for p in range(2)]
        z_ready = sem("z_ready")
        top1_done = sem("top1_done")
        h1_ready = sem("h1_ready")
        top2_done = sem("top2_done")
        h2_ready = sem("h2_ready")
        y_done = sem("y_done")
        y_ready = sem("y_ready")
        last1_done, last1_ready = sem("last1_done"), sem("last1_ready")
        last2_done, last2_ready = sem("last2_done"), sem("last2_ready")
        s_out = sem("s_out")

        MOVED = 16 * (HALF + 1)
        prep_bank = [ps_z, ps_1, ps_2, ps_s]
        base_bank = [*prep_bank, ps_t[0][0], ps_t[0][1], ps_t[1][0], ps_t[1][1]]

        DENSE_TURNS = [range(t, t + 4) for t in range(0, TILES, 4)]
        W2_TURNS = [range(d, min(d + 4, FIELDS)) for d in range(0, FIELDS, 4)]
        FIRST_CW_AT = len(DENSE_TURNS) + len(W2_TURNS) + 1
        cb_own_flat = cb_own[:, :, :, :].rearrange("p s i c -> p s (i c)")
        pieces = [(cb[0], d, ROWS[0], S_0 + 1 + d) for d in range(HALF)]
        pieces += [(cb[1], d, ROWS[1], S_1 + d) for d in range(HALF)]
        pieces += [(cb_own_flat, i, P, S_OWN + i) for i in range(OWN_SLOTS)]
        CW_TURNS = [range(*r) for r in ((0, 3), (3, 6), (6, 9), (9, 13), (13, 16), (16, 19), (19, 22), (22, 25), (25, 26),
                                        (26, 29), (29, 32), (32, 35))]
        OWN_TURN = 9
        assert all((FIRST_CW_AT + i) % 4 for i in range(OWN_TURN, len(CW_TURNS)))
        FIRST_W2 = len(DENSE_TURNS)
        FIRST_BASE = FIRST_W2 + len(W2_TURNS)
        Z1_TURN = FIRST_BASE
        FIRST_CW = FIRST_CW_AT
        PREP = FIRST_CW + len(CW_TURNS)
        z1_pieces = [(w1o[n][:, :], Z1_ROWS[n], w1t[0:Z1_ROWS[n], n, :]) for n in range(2)]
        z1_pieces += [(w1x[:, 0:GX[0]], GX[0], wgx[:, :])]

        block = ctx.enter_context(nc.Block())

        @block.sync
        def _(sp):
            sp.dma_start(idx[0][:, :], ids[0:P, :]).then_inc(s_idx0, 16)
            sp.dma_start(w1r[:, :, :], w1).then_inc(s_w1, 16)
            sp.dma_start(w2r, w2).then_inc(s_w2, 16)
            sp.dma_start(ids_all[:, :, :], ids.rearrange("(t p) f -> p t f", p=P)).then_inc(s_ids, 16)
            for i, f in enumerate(HOT):
                sp.dma_start(hot_n[i], tables[f].rearrange("(p c) d -> p c d", c=HOT_ROWS)).then_inc(s_hot, 16)
            sp.dma_start(wt1[:, :, :], w_top1[0:2 * P, :].rearrange("(c p) n -> p c n", p=P)).then_inc(s_top, 16)
            for row, _, _ in STACK:
                sp.dma_start(wd[row:row + DENSE, :], w_top1[2 * P:, :]).then_inc(s_wd, 16)
            sp.dma_start(wt2[:, :, :], w_top2.rearrange("(c p) n -> p c n", p=P)).then_inc(s_top, 16)
            with nc.allow_non_contiguous_dma(reason="a few hundred biases, once"):
                sp.dma_start(wt3[:, :], w_top3.rearrange("(c p) a -> p (c a)", p=P)).then_inc(s_top, 16)
                sp.dma_start(bt1[:, :], b_top1.rearrange("(c p) -> p c", p=P)).then_inc(s_top, 16)
                sp.dma_start(bt2[:, :], b_top2.rearrange("(c p) -> p c", p=P)).then_inc(s_top, 16)
            sp.dma_start(b2c[:, :], b2.rearrange("(p a) -> p a", a=1)).then_inc(s_top, 16)

            def move_gx(k, p):
                sp.wait_ge(t_copied[0], GROUPS * (2 * k + p + 1))
                wait(sp, z_done[p], k)
                places = [gx[p], tt[p][:, SLOT_ONE[1], :], tt[p][:, SLOT_ONE[0], :]]
                for i, place in enumerate(places):
                    row, end = GX_FIRST[i], GX_FIRST[i] + GX[i]
                    while row < end:
                        d, a = row // HALF, row % HALF
                        count, at = min(HALF - a, end - row), GX_AT[i] + row - GX_FIRST[i]
                        sp.dma_start(place[at:at + count, :],
                                     tt[p][E_AT + a:E_AT + a + count, S_0 + 1 + d, :]).then_inc(gx_ready[p], 16)
                        row += count

            for p in range(2):
                move_gx(0, p)
            with nc.sync.Fori(1, TILES // 2) as k:
                for p in range(2):
                    move_gx(k, p)
            sp.wait_ge(y_ready, TILES)
            sp.dma_start(out.rearrange("b a -> a b"), y[:, :]).then_inc(s_out, 16)
            sp.wait_ge(s_out, 16)

        @block.gpsimd
        def _(pool):
            nc.gpsimd.memset(ident[:, :], 0.0).then_inc(s_ident0, 1)
            pool.wait_ge(s_ident0, 1)
            nc.gpsimd.affine_select(out=ident[:, :], in_=ident[:, :], compare_op=ALU.not_equal, fill=1.0, base=0,
                                    pattern=[[-1, P]], channel_multiplier=1).then_inc(s_ident, 1)
            nc.gpsimd.iota(row_i[:, :], pattern=[[1, HOT_ROWS]], base=0, channel_multiplier=HOT_ROWS
                           ).then_inc(s_rows, 1)

            def gather(p, hot):
                for f in range(FIELDS):
                    if f in HOT and not hot:
                        continue
                    pool.indirect_dma_start(
                        out=gathered[p][:, f * DIM:(f + 1) * DIM], out_offset=None, in_=tables[f],
                        in_offset=bass.IndirectOffsetOnAxis(ap=idx[p][:, f:f + 1], axis=0),
                    ).then_inc(gather_done[p][f // HALF], 16)

            pool.wait_ge(s_idx0, 16)
            gather(0, True)
            pool.wait_ge(idx_ready[1], 1)
            pool.wait_ge(s_parts, 5)
            gather(1, True)
            with nc.gpsimd.Fori(1, TILES // 2) as k:
                for p in range(2):
                    pool.wait_ge(idx_ready[p], k + p)
                    pool.wait_ge(et_ready[p], 2 * k)
                    nc.gpsimd.sem_inc(tile_begun, 1)
                    gather(p, False)

        @block.vector
        def _(dve):
            def next_indices(t, p):
                nc.vector.tensor_copy(idx[p][:, :], ids_all[:, bass.ds(t, 1), :].rearrange("p a f -> p (a f)")
                                      ).then_inc(idx_ready[p], 1)

            def diagonal_ones(p):
                for q in range(QUADS):
                    last = nc.vector.memset(bd[p][q * DIM:(q + 1) * DIM, :, q, C_ONE:C_ONE + 1], 1.0)
                last.then_inc(s_const, 1)

            nc.vector.memset(dense_s, 0.0).then_inc(s_parts, 1)
            dve.wait_ge(s_dense, 16)
            nc.vector.tensor_copy(dense_part[0], dense_n).then_inc(s_parts, 1)
            dve.wait_ge(s_parts, 2)
            for row, part, _ in STACK:
                if part == 0:
                    nc.vector.tensor_copy(dense_s[:, :, row:row + DENSE], dense_part[0])
            nc.vector.tensor_tensor(dense_n, dense_n, dense_part[0], ALU.subtract).then_inc(s_parts, 1)
            dve.wait_ge(s_parts, 3)
            nc.vector.tensor_copy(dense_part[1], dense_n).then_inc(s_parts, 1)
            dve.wait_ge(s_parts, 4)
            for row, part, _ in STACK:
                if part == 1:
                    nc.vector.tensor_copy(dense_s[:, :, row:row + DENSE], dense_part[1])
            nc.vector.tensor_tensor(dense_s[:, :, 2 * DENSE:3 * DENSE], dense_n, dense_part[1], ALU.subtract
                                    ).then_inc(s_parts, 1)

            nc.vector.memset(w1z[:, :], 0.0).then_inc(s_w1s, 1)
            dve.wait_ge(s_w1, 32)
            nc.vector.tensor_tensor(w1q[:, :, :], w1r[:, :, :], w1r[:, :, :].rearrange("p x y -> p y x"),
                                    ALU.add).then_inc(s_w1s, 1)
            dve.wait_ge(s_w1s, 2)
            diag = slice(0, FIELDS * FIELDS, FIELDS + 1)
            nc.vector.tensor_copy(w1q[:, :, :].rearrange("p x y -> p (x y)")[:, diag],
                                  w1r[:, :, :].rearrange("p x y -> p (x y)")[:, diag]).then_inc(s_w1s, 1)
            dve.wait_ge(s_w1s, 3)
            for n in range(2):
                f0 = n * HALF
                for q in range(HALF):
                    row, p0 = within_row(q)
                    at = BASE[n] + row
                    nc.vector.tensor_copy(w1z[:, at:at + q - p0 + 1], w1q[:, f0 + q, f0 + p0:f0 + q + 1])
                for row, (q0, q1), (p0, p1) in CROSS:
                    at = BASE[n] + X_AT + row
                    nc.vector.tensor_copy(w1z[:, at:at + (q1 - q0) * (p1 - p0)].rearrange("p (y x) -> p y x", x=p1 - p0),
                                          w1q[:, f0 + q0:f0 + q1, f0 + p0:f0 + p1])
            nc.vector.tensor_copy(w1x[:, :].rearrange("p (d a) -> p d a", a=HALF), w1q[:, HALF:, 0:HALF])
            nc.vector.tensor_copy(w1z[:, ONE_AT:ONE_AT + 1], b1c[:, :]).then_inc(s_w1s, 1)
            dve.wait_ge(s_w1s, 4)
            for n in range(2):
                first = GX_FIRST[2 - n]
                nc.vector.tensor_copy(w1o[n][:, 0:ROWS[n]], w1z[:, BASE[n]:BASE[n] + ROWS[n]])
                nc.vector.tensor_copy(w1o[n][:, ROWS[n]:], w1x[:, first:first + GX[2 - n]])
            nc.vector.tensor_copy(w1p[:, :], w1z[:, :]).then_inc(s_w1s, 1)
            dve.wait_ge(s_w1s, 5)
            at = BASE[1] + ONE_AT
            nc.vector.tensor_copy(w1p[:, at:at + 1], b1c[:, :]).then_inc(s_w1s, 1)
            dve.wait_ge(s_w1s, 6)
            for n in range(2):
                own, other = (slice(m * HALF, (m + 1) * HALF) for m in (n, 1 - n))
                f0 = n * HALF

                def terms(w, at, ys, ds, width=None, place=0):
                    (y0, y1), (d0, d1) = ys, ds
                    width = width or d1 - d0
                    nc.vector.tensor_copy(
                        w[:, at:at + (y1 - y0) * width].rearrange(
                            "p (y d) -> p y d", d=width)[:, :, place:place + d1 - d0],
                        w1q[:, f0 + y0:f0 + y1, f0 + d0:f0 + d1])
                    return at + (y1 - y0) * width

                for g, (a, b) in enumerate(GROUP_OF):
                    w, at = wpack[n][g // 2], 0 if g % 2 == 0 else SPEC[g - 1] + COMMON[n]
                    for d0, d1, place in others(g):
                        end = terms(w, at, (a, b), (d0, d1), HALF - (b - a), place)
                    at = end
                    if g < 2:
                        at = terms(w, at, GROUP_OF[1 - g], (U0, HALF))
                        at = terms(w, at, (U0, V0), (V0, HALF))
                    elif g == 2:
                        at = terms(w, at, (K0, U0), (V0, HALF))
                    if g >= 2:
                        x = BASE[n] + X_AT
                        nc.vector.tensor_copy(w[:, at:at + KEPT], w1z[:, x:x + KEPT])
                for i in range(2):
                    w = wpack[n][i][:, SPEC[2 * i]:SPEC[2 * i] + COMMON[n]]
                    nc.vector.tensor_copy(w[:, AT_OWN[n]:AT_FH[n]], w1z[:, BASE[n]:BASE[n] + WITHIN])
                    nc.vector.tensor_copy(w[:, AT_FH[n]:COMMON[n]].rearrange("p (y d) -> p y d", d=HALF),
                                          w1q[:, own, other])
                    last = nc.vector.tensor_copy(w[:, 0:ROWS[1 - n]], w1p[:, BASE[1 - n]:BASE[1 - n] + ROWS[1 - n]])
            last.then_inc(s_w1p, 1)
            dve.wait_ge(s_ids, 16)
            next_indices(1, 1)
            dve.wait_ge(s_const, 1)
            diagonal_ones(0)
            nc.vector.memset(cb_own[:, :, :, WITHIN:], 0.0)
            slot = own_block(0, HALF)[0]
            nc.vector.memset(cb_own[:, slot:, 1::2, KEPT:WITHIN], 0.0)
            nc.vector.memset(cb_own[:, slot:slot + V0 - U0, 1::2, KL:KEPT], 0.0)
            dve.wait_ge(s_prep_ps, FIRST_W2)
            for h in range(2):
                for n in range(2):
                    at = BASE[n] + ONE_AT
                    last = nc.vector.memset(prod[h][:, :, at:at + 1], 1.0)
            last.then_inc(s_prodc, 1)

            def fold(second):
                for q in range(HALF):
                    row, p0 = within_row(q)
                    count = q - p0 + 1 - second
                    if count:
                        o = cb_all[:, :, :, row:row + count]
                        if second:
                            term = fold_half[:, :, q, p0:q, :].rearrange("p n y d -> p n d y")
                        else:
                            term = fold_half[:, :, p0:q + 1, q, :].rearrange("p n x d -> p n d x")
                        nc.vector.tensor_tensor(o, o, term, ALU.add)
                for row, (q0, q1), (p0, p1) in CROSS:
                    for n in range(2):
                        o = cb[n][:, :, X_AT + row:X_AT + row + (q1 - q0) * (p1 - p0)].rearrange(
                            "p d (y x) -> p d y x", x=p1 - p0)
                        if second:
                            term = fold_half[:, n, q0:q1, p0:p1, :].rearrange("p x y d -> p d x y")
                        else:
                            term = fold_half[:, n, p0:p1, q0:q1, :].rearrange("p x y d -> p d y x")
                        last = nc.vector.tensor_tensor(o, o, term, ALU.add)
                last.then_inc(s_fold, 1)

            def fold_kept(second):
                for q in range(HALF):
                    row, p0 = within_row(q)
                    g, count = group(q), q - p0 + 1 - second
                    if not count:
                        continue
                    size = GROUP_OF[g][1] - p0
                    fo = fold_own(p0, p0 + size, 0, TERMS_W[g]).rearrange("p n x (y d) -> p n x y d", y=size)
                    if second:
                        term = fo[:, :, q - p0, 0:q - p0, :].rearrange("p n y d -> p n d y")
                    else:
                        term = fo[:, :, 0:q - p0 + 1, q - p0, :].rearrange("p n x d -> p n d x")
                    for d0, d1, place in others(g):
                        slot, i = own_block(0, d0)
                        o = cb_own[:, slot:slot + d1 - d0, i::2, row:row + count].rearrange("p s n c -> p n s c")
                        nc.vector.tensor_tensor(o, o, term[:, :, place:place + d1 - d0, :], ALU.add)
                xs, ys = (GROUP_OF[1], GROUP_OF[0]) if second else (GROUP_OF[0], GROUP_OF[1])
                at = TERMS_W[int(second)]
                slot = own_block(0, HALF)[0]
                for n in range(2):
                    term = fold_own(*xs, at, at + (ys[1] - ys[0]) * (HALF - U0))[:, n, :, :].rearrange(
                        "p x (y d) -> p x y d", d=HALF - U0).rearrange(
                            "p x y d -> p d x y" if second else "p x y d -> p d y x")
                    o = cb_own[:, slot:, own_block(n, HALF)[1], 0:KL].rearrange("p d (y x) -> p d y x", x=L0 - K0)
                    nc.vector.tensor_tensor(o, o, term, ALU.add)
                if second:
                    term = fold_own(U0, V0, TERMS_W[2], TERMS[2]).rearrange("p n x (y d) -> p n (x d) y", d=HALF - V0)
                else:
                    term = fold_own(K0, U0, TERMS[0] - (HALF - V0), TERMS[0]).rearrange("p n x d -> p n d x")
                o = cb_own[:, slot + V0 - U0:, 1::2, KL:KEPT].rearrange("p s n c -> p n s c")
                last = nc.vector.tensor_tensor(o, o, term, ALU.add)
                last.then_inc(s_fold, 1)

            def products(h, n, e):
                f0 = n * HALF
                for q in range(HALF):
                    row, p0 = within_row(q)
                    at, count = BASE[n] + row, q - p0 + 1
                    nc.vector.tensor_tensor(
                        prod[h][:, :, at:at + count], e[:, :, f0 + p0:f0 + q + 1],
                        e[:, :, f0 + q:f0 + q + 1].broadcast_to([P, HR, count]), ALU.mult)
                for row, (q0, q1), (p0, p1) in CROSS:
                    at, ny, nx = BASE[n] + X_AT + row, q1 - q0, p1 - p0
                    last = nc.vector.tensor_tensor(
                        prod[h][:, :, at:at + ny * nx].rearrange("p r (y x) -> p r y x", x=nx),
                        e[:, :, f0 + p0:f0 + p1].unsqueeze(2).broadcast_to([P, HR, ny, nx]),
                        e[:, :, f0 + q0:f0 + q1].unsqueeze(3).broadcast_to([P, HR, ny, nx]), ALU.mult)
                return last

            def pick_ids(t):
                nc.vector.tensor_copy(hot_ids[:, :, :], ids_all[:, bass.ds(t, 1), HOT_FIELDS].rearrange(
                    "p a f -> p (a f)").unsqueeze(2).broadcast_to([P, HOTS, HOT_P])).then_inc(hot_ids_ready, 1)

            def pick_rows(t, p):
                count = t - FIRST_HOT + 1
                dve.wait_ge(ids_spread, count)
                for j in range(HOTS):
                    last = nc.vector.tensor_tensor(
                        one_hot[:, j, :, :],
                        spread_ps[:, j * P:(j + 1) * P].unsqueeze(1).broadcast_to([HOT_P, HOT_ROWS, P]),
                        row_no[:, :].unsqueeze(2).broadcast_to([HOT_P, HOT_ROWS, P]), ALU.is_equal)
                last.then_inc(one_hot_ready, 1)
                dve.wait_ge(rows_picked, count)
                nc.vector.tensor_reduce(gathered[p][:, :].rearrange("p (f k) -> p f k", k=DIM)[:, HOT_FIELDS, :],
                                        picked_ps.rearrange("s (f i d) -> s f d i", i=PARTS, d=DIM),
                                        axis=mybir.AxisListType.X, op=ALU.add).then_inc(rows_placed, 1)

            def field_half(k, p, n, hot):
                t = 2 * k + p
                if n == 0:
                    wait(dve, bd_ready[p], 2 * k)
                    wait(dve, prod_ready[1], t)
                    wait(dve, rows_placed, t - FIRST_HOT + 1)
                own = HALF - (HOTS if n == 0 else 0)
                fields = slice(n * HALF, (n + 1) * HALF)
                dve.wait_ge(gather_done[p][n], 16 * HALF + 16 * own * k)
                nc.vector.transpose(et[p][:, :, fields].rearrange("p r f -> p f r"),
                                    gathered[p][:, n * HALF * DIM:(n + 1) * HALF * DIM].rearrange(
                                        "p (f k) -> p f k", k=DIM)).then_inc(et_ready[p], 1)
                if n == 1 and (not isinstance(k, int) or k < TILES // 2 - 1):
                    next_indices(t + 2, p)
                if n == 1 and hot:
                    pick_ids(t + 1)
                dve.wait_ge(et_ready[p], 2 * k + n + 1)
                for h in range(2):
                    e = et[p][:, h * HR:(h + 1) * HR, :]
                    if n == 0:
                        wait(dve, t_done[1], GROUPS * t - GPH * (1 - h))
                        nc.vector.tensor_copy(prod[h][:, :, E_AT:E_AT + HALF], e[:, :, 0:HALF])
                    last = products(h, n, e)
                    if n == 1:
                        last.then_inc(prod_ready[h], 1)

            def tile(k, p):
                for n in range(2):
                    field_half(k, p, n, True)
                pick_rows(2 * k + p + 1, 1 - p)

            field_half(0, 0, 0, False)
            dve.wait_ge(s_prep_ps, FIRST_BASE)
            nc.vector.memset(bd[1][:, :, :, :], 0.0).then_inc(s_const, 1)
            dve.wait_ge(s_const, 3)
            diagonal_ones(1)

            dve.wait_ge(s_hot, 16 * HOTS)
            for i in range(PARTS):
                for j in range(HOTS):
                    last = nc.vector.tensor_copy(hot_table[:, j, :, i, :], hot_n[j])
                last.then_inc(s_hot_parts, 1)
                dve.wait_ge(s_hot_parts, 2 * i + 1)
                if i < PARTS - 1:
                    for j in range(HOTS):
                        last = nc.vector.tensor_tensor(hot_n[j], hot_n[j], hot_table[:, j, :, i, :], ALU.subtract)
                    last.then_inc(s_hot_parts, 1)
                    dve.wait_ge(s_hot_parts, 2 * i + 2)
            dve.wait_ge(s_rows, 1)
            nc.vector.tensor_copy(row_no[:, :], row_i[:, :]).then_inc(s_hot_parts, 1)
            dve.wait_ge(s_ident, 1)
            nc.vector.tensor_copy(ident16[:, :], ident[:, :]).then_inc(s_hot_parts, 1)

            field_half(0, 0, 1, False)
            dve.wait_ge(s_base_ev, FIELDS)
            for step, passes in enumerate((fold, fold, fold_kept, fold_kept)):
                wait(dve, s_fold, step)
                passes(step % 2)
            field_half(0, 1, 0, True)
            field_half(0, 1, 1, True)

            lower, last_part = slice(64, STACK_ROWS), slice(96, STACK_ROWS)
            nc.vector.memset(wt1d[32:64, :], 0.0).then_inc(s_wparts, 1)
            dve.wait_ge(s_wd, 16 * len(STACK))
            dve.wait_ge(s_wparts, 1)
            nc.vector.tensor_copy(wt1d[0:3 * DENSE, :], wd[0:3 * DENSE])
            for i, (rows, left) in enumerate(((lower, lower), (lower, last_part))):
                nc.vector.tensor_copy(wt1d[rows, :], wd[rows]).then_inc(s_wparts, 1)
                dve.wait_ge(s_wparts, 2 * i + 2)
                nc.vector.tensor_tensor(wd[left], wd[left], wt1d[left, :], ALU.subtract).then_inc(s_wparts, 1)
                dve.wait_ge(s_wparts, 2 * i + 3)
            nc.vector.tensor_copy(wt1d[last_part, :], wd[last_part]).then_inc(s_wparts, 1)

            pick_rows(2, 0)
            with nc.vector.Fori(1, TILES // 2 - 1) as k:
                for p in range(2):
                    tile(k, p)
            tile(TILES // 2 - 1, 0)
            for n in range(2):
                field_half(TILES // 2 - 1, 1, n, False)

        @block.scalar
        def _(act):
            act.dma_start(b1c[:, :], b1.rearrange("(p a) -> p a", a=1)).then_inc(s_w1, 16)
            act.dma_start(dense_n, dense.rearrange("(t p) f -> p t f", p=P)).then_inc(s_dense, 16)

            def copy(dst, src):
                return nc.scalar.activation(dst, src, ACT.Copy)

            act.wait_ge(s_ident, 1)
            nc.scalar.activation(bd[0][:, :, :, :].rearrange("p r q s -> p r (q s)"),
                                 ident[:, 0:QUADS * COLS].unsqueeze(1).broadcast_to([P, DIM, QUADS * COLS]),
                                 ACT.Copy, scale=0.0).then_inc(s_const, 1)
            for i, ts in enumerate(DENSE_TURNS):
                act.wait_ge(s_prep_ps, i + 1)
                copy(dense_t[:, ts[0] * P:(ts[-1] + 1) * P],
                     prep_bank[i % 4][0:STACK_ROWS, 0:len(ts) * P]).then_inc(s_prep_ev, 1)
            for i, ds in enumerate(W2_TURNS):
                turn = FIRST_W2 + i
                act.wait_ge(s_prep_ps, turn + 1)
                copy(w2t[:, ds[0]:ds[-1] + 1, :].rearrange("p d h -> p (d h)"),
                     prep_bank[turn % 4][:, 0:len(ds) * P]).then_inc(s_prep_ev, 1)

            def fields_a_out(k, p):
                wait(act, t_done[1], GROUPS * (2 * k + p))
                act.wait_ge(et_ready[p], 2 * k + 1)
                for q in range(QUADS):
                    rows = slice(q * DIM, (q + 1) * DIM)
                    copy(bd[p][rows, :, q, 0:HALF], et[p][rows, :, 0:HALF])

            def fields_b_out(k, p):
                act.wait_ge(et_ready[p], 2 * k + 2)
                for h in range(2):
                    rs = slice(h * HR, (h + 1) * HR)
                    for q in range(QUADS):
                        rows = slice(q * DIM, (q + 1) * DIM)
                        last = copy(bd[p][rows, rs, q, C_B:C_B + HALF], et[p][rows, rs, HALF:])
                    last.then_inc(bd_ready[p], 1)

            for x in range(FIELDS):
                if x == HALF:
                    act.wait_ge(s_const, 2)
                    fields_a_out(0, 0)
                n, q = x // HALF, x % HALF
                g = group(q)
                bank, (common, spec) = base_bank[x % 8], bank_columns(n, g)
                act.wait_ge(s_base_ps, x + 1)
                copy(cb[1 - n][:, q, :], bank[:, common:common + ROWS[1 - n]])
                slot, i = own_block(n, q)
                copy(cb_own[:, slot, i, 0:WITHIN], bank[:, common + AT_OWN[n]:common + AT_FH[n]])
                copy(fold_half[:, n, q, :, :].rearrange("p y d -> p (y d)"),
                     bank[:, common + AT_FH[n]:common + COMMON[n]])
                if g >= 2:
                    kept = KL if g == 2 else KEPT
                    at = spec + TERMS[g]
                    slot, i = own_block(n, HALF + q - U0)
                    copy(cb_own[:, slot, i, 0:kept], bank[:, at:at + kept])
                copy(fold_own(q, q + 1, 0, TERMS[g])[:, n, :, :].rearrange("p x c -> p (x c)"),
                     bank[:, spec:spec + TERMS[g]]).then_inc(s_base_ev, 1)
            fields_b_out(0, 0)
            act.wait_ge(s_prep_ps, Z1_TURN + 1)
            for j, (_, rows, dst) in enumerate(z1_pieces):
                last = copy(dst, prep_bank[Z1_TURN % 4][0:rows, j * P:(j + 1) * P])
            last.then_inc(s_prep_ev, 1)
            act.wait_ge(s_top, 16 * 6)
            nc.scalar.mul(b2k[:, :], b2c[:, :], float(DIM)).then_inc(s_b2, 1)

            def triples_out(k, p):
                wait(act, z_done[p], k)
                wait(act, gx_ready[p], MOVED * k)
                for g in range(GROUPS):
                    b = g % 2
                    samples = slice(g * GR, (g + 1) * GR)
                    parts = [(0, 0, ROWS[0], 0, S_0, C_ONE, HALF + 1), (1, 0, ROWS[1], 0, S_1, 0, HALF + 1)]
                    for n in range(2):
                        c, low, high = n * C_B, 2 * n * BLOCK, (2 * n + 1) * BLOCK
                        left = HALF - OWN_SLOTS
                        parts += [(n, 0, BLOCK, low, S_OWN, c, OWN_SLOTS),
                                  (n, 0, BLOCK, high, S_OWN, c + OWN_SLOTS, left),
                                  (n, X_AT, BLOCK, high, S_OWN + left, c + U0, HALF - U0)]
                    parts.sort()
                    for i, (n, row, rows, at, s0, c0, count) in enumerate(parts):
                        if i == 0 or parts[i - 1][0] != n:
                            act.wait_ge(t_done[n], GROUPS * (2 * k + p) + g + 1)
                        last = copy(
                            tt[p][at:at + rows, s0:s0 + count, :].rearrange(
                                "p s (q r) -> p s q r", q=QUADS)[:, :, :, samples],
                            ps_t[b][n][row:row + rows, 0:GR * QUADS * COLS].rearrange(
                                "p (r q s) -> p s q r", q=QUADS, s=COLS)[:, c0:c0 + count, :, :])
                        if i == len(parts) - 1 or parts[i + 1][0] != n:
                            last.then_inc(t_copied[n], 1)

            def z_out(k, p):
                act.wait_ge(z_done[p], k + 1)
                wait(act, top1_done, 2 * k + p)
                copy(z[:, 0, :], z1_ps)
                nc.scalar.activation(z[:, 1, :], z2_ps, ACT.Identity, bias=b2k[:, 0:1]).then_inc(z_ready, 1)

            def h1_out(t):
                act.wait_ge(top1_done, t + 1)
                wait(act, top2_done, t)
                for m in range(M1):
                    last = nc.scalar.activation(h1[:, m, :], ps_1[:, m * P:(m + 1) * P], ACT.Relu,
                                                bias=bt1[:, m:m + 1])
                last.then_inc(h1_ready, 1)

            def h2_out(t):
                act.wait_ge(top2_done, t + 1)
                wait(act, y_done, t)
                for m in range(M2):
                    last = nc.scalar.activation(h2[:, m, :], ps_2[:, m * P:(m + 1) * P], ACT.Relu,
                                                bias=bt2[:, m:m + 1])
                last.then_inc(h2_ready, 1)

            def y_out(t):
                act.wait_ge(y_done, t + 1)
                copy(y[:, bass.ds(t * P, P)], y_ps).then_inc(y_ready, 1)

            act.wait_ge(s_b2, 1)
            triples_out(0, 0)
            for i, turn_pieces in enumerate(CW_TURNS):
                act.wait_ge(s_prep_ps, FIRST_CW + i + 1)
                bank = prep_bank[(FIRST_CW + i) % 4]
                runs = []
                for j, c in enumerate(turn_pieces):
                    if runs and pieces[runs[-1][0]][2] == pieces[c][2]:
                        runs[-1][2] += 1
                    else:
                        runs.append([c, j, 1])
                for c, j, count in runs:
                    rows = pieces[c][2]
                    last = copy(cw[0:rows, c:c + count, :].rearrange("p s h -> p (s h)"),
                                bank[0:rows, j * P:(j + count) * P])
                last.then_inc(s_prep_ev, 1)
            act.wait_ge(s_const, 4)
            fields_a_out(0, 1)
            fields_b_out(0, 1)
            act.wait_ge(s_hot_parts, 5)
            z_out(0, 0)

            def tile(k, p, t):
                triples_out(k, p)
                h1_out(t - 1)
                fields_a_out(k + p, 1 - p)
                h2_out(t - 1)
                fields_b_out(k + p, 1 - p)
                y_out(t - 1)
                z_out(k, p)

            act.wait_ge(s_fold, 4)
            tile(0, 1, 1)
            tile(1, 0, 2)
            with nc.scalar.Fori(1, TILES // 2 - 1) as k:
                tile(k, 1, 2 * k + 1)
                tile(k + 1, 0, 2 * k + 2)
            triples_out(TILES // 2 - 1, 1)
            h1_out(TILES - 2)
            h2_out(TILES - 2)
            y_out(TILES - 2)
            z_out(TILES // 2 - 1, 1)
            for m in range(M1):
                act.wait_ge(last1_done, m + 1)
                nc.scalar.activation(h1[:, m, :], last1_ps[m], ACT.Relu, bias=bt1[:, m:m + 1]
                                     ).then_inc(last1_ready, 1)
            for m in range(M2):
                act.wait_ge(last2_done, m + 1)
                nc.scalar.activation(h2[:, m, :], last2_ps[m], ACT.Relu, bias=bt2[:, m:m + 1]
                                     ).then_inc(last2_ready, 1)
            act.wait_ge(y_done, TILES)
            copy(y[:, (TILES - 1) * P:], last_y_ps).then_inc(y_ready, 1)

        @block.tensor
        def _(pe):
            def turn_free(turn):
                wait(pe, s_prep_ev, turn - 3)

            pe.wait_ge(s_ident, 1)
            pe.wait_ge(s_parts, 5)
            for i, ts in enumerate(DENSE_TURNS):
                turn_free(i)
                for j, t in enumerate(ts):
                    last = nc.tensor.transpose(prep_bank[i % 4][0:STACK_ROWS, j * P:(j + 1) * P], dense_s[:, t, :],
                                               ident[:, :])
                last.then_inc(s_prep_ps, 1)
            pe.wait_ge(s_w2, 16)
            for i, ds in enumerate(W2_TURNS):
                turn = FIRST_W2 + i
                turn_free(turn)
                for j, d in enumerate(ds):
                    last = nc.tensor.transpose(prep_bank[turn % 4][:, j * P:(j + 1) * P], w2r[:, :, d], ident[:, :])
                last.then_inc(s_prep_ps, 1)
            pe.wait_ge(s_w1p, 1)
            pe.wait_ge(s_prep_ev, FIRST_BASE)
            for x in range(FIELDS):
                n, g = x // HALF, group(x % HALF)
                wait(pe, s_base_ev, x - 7)
                width = SPEC[g] + COMMON[n]
                at = 0 if g % 2 == 0 else SPEC[g - 1]
                nc.tensor.matmul(base_bank[x % 8][:, 0:width], w2t[:, x, :], wpack[n][g // 2][:, at:at + width],
                                 start=True, stop=True).then_inc(s_base_ps, 1)
            pe.wait_ge(s_base_ev, FIELDS)
            turn_free(Z1_TURN)
            for j, (src, rows, _) in enumerate(z1_pieces):
                last = nc.tensor.transpose(prep_bank[Z1_TURN % 4][0:rows, j * P:(j + 1) * P], src, ident[:, :])
            last.then_inc(s_prep_ps, 1)

            def spread_ids(t):
                pe.wait_ge(hot_ids_ready, t - FIRST_HOT + 1)
                wait(pe, one_hot_ready, t - FIRST_HOT)
                for j in range(HOTS):
                    last = nc.tensor.matmul(spread_ps[:, j * P:(j + 1) * P], hot_ids[:, j, :], ident16[:, :],
                                            start=True, stop=True)
                last.then_inc(ids_spread, 1)

            def triples(k, p, hot):
                for g in range(GROUPS):
                    h, b = g // GPH, g % 2
                    if g % GPH == 0:
                        pe.wait_ge(bd_ready[p], 2 * k + h + 1)
                        pe.wait_ge(prod_ready[h], 2 * k + p + 1)
                    for n in range(2):
                        wait(pe, t_copied[n], GROUPS * (2 * k + p) + g - 1)
                        for j in range(GR):
                            r = g * GR + j
                            last = nc.tensor.matmul(
                                ps_t[b][n][0:ROWS[n], j * QUADS * COLS:(j + 1) * QUADS * COLS],
                                prod[h][:, r - h * HR, BASE[n]:BASE[n] + ROWS[n]],
                                bd[p][:, r, :, :].rearrange("p q s -> p (q s)"), start=True, stop=True)
                        last.then_inc(t_done[n], 1)
                    if hot and g == GPH - 1:
                        spread_ids(2 * k + p + 1)

            N_PIECES = len(pieces)

            def z2_part(p, lo, hi):
                for i in range(lo, hi):
                    _, _, rows, s = pieces[i]
                    nc.tensor.matmul(z2_ps, cw[0:rows, i, :], tt[p][0:rows, s, :],
                                     start=(i == 0), stop=(i == N_PIECES - 1))

            def z_begin(k, p):
                for n in range(2):
                    pe.wait_ge(t_copied[n], GROUPS * (2 * k + p + 1))
                wait(pe, z_ready, 2 * k + p)

            def z1_part(k, p):
                pe.wait_ge(gx_ready[p], MOVED * (k + 1))
                nc.tensor.matmul(z1_ps, wgx[:, :], gx[p][:, :], start=True, stop=False)
                for n in range(2):
                    last = nc.tensor.matmul(z1_ps, w1t[0:Z1_ROWS[n], n, :], tt[p][0:Z1_ROWS[n], SLOT_ONE[n], :],
                                            start=False, stop=(n == 1))
                last.then_inc(z_done[p], 1)

            def top1(t):
                if isinstance(t, int) and t == 0:
                    pe.wait_ge(s_wparts, 6)
                pe.wait_ge(z_ready, t + 1)
                wait(pe, h1_ready, t)
                for m in range(M1):
                    cols = slice(m * P, (m + 1) * P)
                    nc.tensor.matmul(ps_1[:, cols], wt1d[:, cols], dense_t[:, bass.ds(t * P, P)],
                                     start=True, stop=False)
                    nc.tensor.matmul(ps_1[:, cols], wt1[:, 0, cols], z[:, 0, :], start=False, stop=False)
                    last = nc.tensor.matmul(ps_1[:, cols], wt1[:, 1, cols], z[:, 1, :], start=False, stop=True)
                last.then_inc(top1_done, 1)

            def top2(t):
                pe.wait_ge(h1_ready, t + 1)
                wait(pe, h2_ready, t)
                wait(pe, y_ready, t)
                for m in range(M2):
                    for c in range(M1):
                        last = nc.tensor.matmul(ps_2[:, m * P:(m + 1) * P], wt2[:, c, m * P:(m + 1) * P], h1[:, c, :],
                                                start=(c == 0), stop=(c == M1 - 1))
                last.then_inc(top2_done, 1)

            def top3(t):
                pe.wait_ge(h2_ready, t + 1)
                for c in range(M2):
                    last = nc.tensor.matmul(y_ps, wt3[:, c:c + 1], h2[:, c, :], start=(c == 0), stop=(c == M2 - 1))
                last.then_inc(y_done, 1)

            def pick_rows(t):
                pe.wait_ge(one_hot_ready, t - FIRST_HOT + 1)
                wait(pe, rows_placed, t - FIRST_HOT)
                for j in range(HOTS):
                    for c in range(HOT_ROWS):
                        last = nc.tensor.matmul(picked_ps[:, j * PARTS * DIM:(j + 1) * PARTS * DIM], one_hot[:, j, c, :],
                                                hot_table[:, j, c, :, :].rearrange("p i d -> p (i d)"),
                                                start=(c == 0), stop=(c == HOT_ROWS - 1))
                last.then_inc(rows_picked, 1)

            def tile(k, p, t, hot=True):
                triples(k, p, hot)
                if hot:
                    pick_rows(t + 1)
                top1(t - 1)
                z_begin(k, p)
                z2_part(p, 0, N_PIECES // 2)
                top2(t - 1)
                z2_part(p, N_PIECES // 2, N_PIECES * 3 // 4)
                top3(t - 1)
                z2_part(p, N_PIECES * 3 // 4, N_PIECES)
                z1_part(k, p)

            pe.wait_ge(s_prodc, 1)
            triples(0, 0, False)
            def weights_turned(turns):
                for i in turns:
                    turn = FIRST_CW + i
                    pe.wait_ge(s_fold, 2 if i < OWN_TURN else 4)
                    turn_free(turn)
                    for j, c in enumerate(CW_TURNS[i]):
                        src, d, rows, _ = pieces[c]
                        last = nc.tensor.transpose(prep_bank[turn % 4][0:rows, j * P:(j + 1) * P], src[:, d, :],
                                                   ident[:, :])
                    last.then_inc(s_prep_ps, 1)

            weights_turned(range(OWN_TURN))
            pe.wait_ge(s_prep_ev, FIRST_CW + OWN_TURN)
            z_begin(0, 0)
            z2_part(0, 0, HALF)
            weights_turned(range(OWN_TURN, len(CW_TURNS)))
            z2_part(0, HALF, 2 * HALF)
            pe.wait_ge(s_prep_ev, PREP)
            z2_part(0, 2 * HALF, N_PIECES)
            z1_part(0, 0)
            pe.wait_ge(s_top, 16 * 6)
            pe.wait_ge(s_hot_parts, 7)
            tile(0, 1, 1)
            tile(1, 0, 2)
            with nc.tensor.Fori(1, TILES // 2 - 1) as k:
                tile(k, 1, 2 * k + 1)
                tile(k + 1, 0, 2 * k + 2)
            tile(TILES // 2 - 1, 1, TILES - 1, hot=False)
            for m in range(M1):
                nc.tensor.matmul(last1_ps[m], wt1d[:, m * P:(m + 1) * P], dense_t[:, (TILES - 1) * P:],
                                 start=True, stop=False)
            pe.wait_ge(z_ready, TILES)
            for m in range(M1):
                cols = slice(m * P, (m + 1) * P)
                nc.tensor.matmul(last1_ps[m], wt1[:, 0, cols], z[:, 0, :], start=False, stop=False)
                nc.tensor.matmul(last1_ps[m], wt1[:, 1, cols], z[:, 1, :], start=False, stop=True
                                 ).then_inc(last1_done, 1)
            pe.wait_ge(h1_ready, TILES - 1)
            pe.wait_ge(h2_ready, TILES - 1)
            pe.wait_ge(y_ready, TILES - 1)
            for m in range(M2):
                for c in range(M1):
                    if m == 0:
                        pe.wait_ge(last1_ready, c + 1)
                    last = nc.tensor.matmul(last2_ps[m], wt2[:, c, m * P:(m + 1) * P], h1[:, c, :],
                                            start=(c == 0), stop=(c == M1 - 1))
                last.then_inc(last2_done, 1)
            pe.wait_ge(rows_placed, TILES - FIRST_HOT)
            for c in range(M2):
                pe.wait_ge(last2_ready, c + 1)
                last = nc.tensor.matmul(last_y_ps, wt3[:, c:c + 1], h2[:, c, :], start=(c == 0), stop=(c == M2 - 1))
            last.then_inc(y_done, 1)


TABLES = [f"tbl_{f}" for f in range(FIELDS)]
INPUTS = ["dense_ctx", "ids", *TABLES, "W_top1", "b_top1", "W_top2", "b_top2", "W_top3",
          "L0_rec_W1", "L0_rec_b1", "L0_rec_W2", "L0_rec_b2"]


def kernel(**inputs):
    import numpy as np
    import concourse.bacc as bacc
    from concourse import mybir
    from concourse.bass_utils import run_bass_kernel_spmd

    nc = bacc.Bacc("TRN2", target_bir_lowering=False, num_devices=1)
    arrays, ap = {}, {}
    for name in INPUTS:
        a = np.ascontiguousarray(inputs[name])
        arrays[f"in_{name}"] = a
        ap[name] = nc.dram_tensor(f"in_{name}", a.shape, mybir.dt.from_np(a.dtype), kind="ExternalInput").ap()
    out = nc.dram_tensor("out", (BATCH, 1), mybir.dt.float32, kind="ExternalOutput").ap()
    build(nc, ap["dense_ctx"], ap["ids"], [ap[t] for t in TABLES], ap["W_top1"], ap["b_top1"], ap["W_top2"],
          ap["b_top2"], ap["W_top3"], ap["L0_rec_W1"], ap["L0_rec_b1"], ap["L0_rec_W2"], ap["L0_rec_b2"], out)
    result = run_bass_kernel_spmd(nc, [arrays], core_ids=[0])
    return result.results[0]["out"]
```
